# Optimizing a Trainium2 kernel written in Bass

```python
import numpy as np
import jax
import jax.numpy as jnp

def _softmax(x, axis=-1):
    return jax.nn.softmax(x, axis=axis)

def _gelu(x):
    return jax.nn.gelu(x, approximate=True)

def _silu(x):
    return jax.nn.silu(x)

def _sigmoid(x):
    return jax.nn.sigmoid(x)

def _layernorm(x, axis=-1, eps=1e-05):
    m = jnp.mean(x, axis=axis, keepdims=True)
    v = jnp.var(x, axis=axis, keepdims=True)
    return (x - m) / jnp.sqrt(v + eps)

def _scatter_add(tgt, idx, src, axis=0):
    return tgt.at[idx].add(src)

def _segment_sum(src, seg, n):
    return jax.ops.segment_sum(src, seg, n)
kernel_name = 'mk_conv_seq_d1_conv_nhwc256_r2_4ada1e'

def setup_inputs(seed: int=0):
    np.random.seed(seed)
    _w = jnp.asarray

    def _rec_inputs():
        import jax
        import jax.numpy as jnp
        _gk = jax.random.key(seed)
        x = -0.0003929 + 0.9999 * jax.random.normal(jax.random.fold_in(_gk, 1), (16, 32, 32, 128), jnp.float32)
        return x
    x = _rec_inputs()

    def _L0_conv_setup():
        import jax, jax.numpy as jnp
        import numpy as np
        B, H, W, DIM = (16, 32, 32, 128)
        EXPAND = 2
        D_INNER = DIM * EXPAND
        HID = D_INNER // 2

        def _resize_linear_axis(x, out_size, axis):
            in_size = x.shape[axis]
            scale = in_size / out_size
            src = (jnp.arange(out_size, dtype=jnp.float32) + 0.5) * scale - 0.5
            src = jnp.clip(src, 0.0, in_size - 1)
            i0 = jnp.floor(src).astype(jnp.int32)
            i1 = jnp.minimum(i0 + 1, in_size - 1)
            w = src - i0.astype(jnp.float32)
            x0 = jnp.take(x, i0, axis=axis)
            x1 = jnp.take(x, i1, axis=axis)
            shape = [1] * x.ndim
            shape[axis] = out_size
            w = w.reshape(shape)
            return x0 * (1.0 - w) + x1 * w

        def _avgpool3_mean(g):
            s = jax.lax.reduce_window(g, 0.0, jax.lax.add, (1, 1, 3, 3), (1, 1, 1, 1), [(0, 0), (0, 0), (1, 1), (1, 1)])
            return (s / 9.0).mean(axis=(2, 3))

        def _gru_dir(xp, whh, bhh, reverse):
            hid = whh.shape[1]
            h0 = jnp.zeros((xp.shape[0], hid), xp.dtype)

            def step(h, xt):
                gh = h @ whh.T + bhh
                xr, xz, xn = jnp.split(xt, 3, axis=-1)
                hr, hz, hn = jnp.split(gh, 3, axis=-1)
                r = jax.nn.sigmoid(xr + hr)
                z = jax.nn.sigmoid(xz + hz)
                n = jnp.tanh(xn + r * hn)
                h_new = (1.0 - z) * n + z * h
                return (h_new, h_new)
            _, ys = jax.lax.scan(step, h0, jnp.swapaxes(xp, 0, 1), reverse=reverse)
            return jnp.swapaxes(ys, 0, 1)

        def _forward(x, ln_gamma, ln_beta, mlp_w1, mlp_b1, mlp_w2, mlp_b2, in_w, in_b, gru_wih_f, gru_whh_f, gru_bih_f, gru_bhh_f, gru_wih_b, gru_whh_b, gru_bih_b, gru_bhh_b, out_w, out_b):
            Bx, Hx, Wx, C = x.shape
            mu = x.mean(-1, keepdims=True)
            var = ((x - mu) ** 2).mean(-1, keepdims=True)
            xn = (x - mu) / jnp.sqrt(var + 1e-05) * ln_gamma + ln_beta
            gray = xn.mean(-1)[:, None]
            gp = jnp.pad(gray, ((0, 0), (0, 0), (1, 1), (1, 1)), mode='reflect')
            grad_h = jnp.abs(gp[:, :, :, 2:] - gp[:, :, :, :-2])
            grad_v = jnp.abs(gp[:, :, 2:, :] - gp[:, :, :-2, :])
            grad_h = _resize_linear_axis(grad_h, Hx, axis=2)
            grad_v = _resize_linear_axis(grad_v, Wx, axis=3)
            grad_d = (grad_h + grad_v) * 0.5
            grad_a = jnp.abs(grad_h - grad_v)
            scores = jnp.concatenate([_avgpool3_mean(g) for g in (grad_h, grad_v, grad_d, grad_a)], axis=1)
            h1 = jax.nn.relu(scores @ mlp_w1.T + mlp_b1)
            logits = h1 @ mlp_w2.T + mlp_b2
            probs = jax.nn.softmax(logits, axis=-1)
            idx = jnp.argmax(probs, axis=-1)
            seq_h = xn.reshape(Bx, Hx * Wx, C)
            seq_v = jnp.swapaxes(xn, 1, 2).reshape(Bx, Hx * Wx, C)
            seq = jnp.where((idx == 1)[:, None, None], seq_v, seq_h)
            z = seq @ in_w.T + in_b
            yf = _gru_dir(z @ gru_wih_f.T + gru_bih_f, gru_whh_f, gru_bhh_f, False)
            yb = _gru_dir(z @ gru_wih_b.T + gru_bih_b, gru_whh_b, gru_bhh_b, True)
            y = jnp.concatenate([yf, yb], axis=-1) @ out_w.T + out_b
            return x + y.reshape(Bx, Hx, Wx, C)
        ks = jax.random.split(jax.random.key(seed), 10)
        g = lambda i, shape, s=0.05: jax.random.normal(ks[i], shape, dtype=jnp.float32) * s
        return {'x': jax.random.normal(ks[0], (B, H, W, DIM), dtype=jnp.float32), 'ln_gamma': jnp.ones((DIM,), jnp.float32), 'ln_beta': jnp.zeros((DIM,), jnp.float32), 'mlp_w1': g(1, (32, 4), 0.3), 'mlp_b1': jnp.zeros((32,), jnp.float32), 'mlp_w2': g(2, (4, 32), 0.3), 'mlp_b2': jnp.zeros((4,), jnp.float32), 'in_w': g(3, (D_INNER, DIM)), 'in_b': jnp.zeros((D_INNER,), jnp.float32), 'gru_wih_f': g(4, (3 * HID, D_INNER)), 'gru_whh_f': g(5, (3 * HID, HID)), 'gru_bih_f': jnp.zeros((3 * HID,), jnp.float32), 'gru_bhh_f': jnp.zeros((3 * HID,), jnp.float32), 'gru_wih_b': g(6, (3 * HID, D_INNER)), 'gru_whh_b': g(7, (3 * HID, HID)), 'gru_bih_b': jnp.zeros((3 * HID,), jnp.float32), 'gru_bhh_b': jnp.zeros((3 * HID,), jnp.float32), 'out_w': g(8, (DIM, D_INNER)), 'out_b': jnp.zeros((DIM,), jnp.float32)}
    _L0_conv_all = _L0_conv_setup()
    _L0_conv_in = {k: v for k, v in _L0_conv_all.items() if k in ('ln_gamma', 'ln_beta', 'mlp_w1', 'mlp_b1', 'mlp_w2', 'mlp_b2', 'in_w', 'in_b', 'gru_wih_f', 'gru_whh_f', 'gru_bih_f', 'gru_bhh_f', 'gru_wih_b', 'gru_whh_b', 'gru_bih_b', 'gru_bhh_b', 'out_w', 'out_b')}
    del _L0_conv_all
    return {'x': x, 'L0_conv_ln_gamma': _L0_conv_in['ln_gamma'], 'L0_conv_ln_beta': _L0_conv_in['ln_beta'], 'L0_conv_mlp_w1': _L0_conv_in['mlp_w1'], 'L0_conv_mlp_b1': _L0_conv_in['mlp_b1'], 'L0_conv_mlp_w2': _L0_conv_in['mlp_w2'], 'L0_conv_mlp_b2': _L0_conv_in['mlp_b2'], 'L0_conv_in_w': _L0_conv_in['in_w'], 'L0_conv_in_b': _L0_conv_in['in_b'], 'L0_conv_gru_wih_f': _L0_conv_in['gru_wih_f'], 'L0_conv_gru_whh_f': _L0_conv_in['gru_whh_f'], 'L0_conv_gru_bih_f': _L0_conv_in['gru_bih_f'], 'L0_conv_gru_bhh_f': _L0_conv_in['gru_bhh_f'], 'L0_conv_gru_wih_b': _L0_conv_in['gru_wih_b'], 'L0_conv_gru_whh_b': _L0_conv_in['gru_whh_b'], 'L0_conv_gru_bih_b': _L0_conv_in['gru_bih_b'], 'L0_conv_gru_bhh_b': _L0_conv_in['gru_bhh_b'], 'L0_conv_out_w': _L0_conv_in['out_w'], 'L0_conv_out_b': _L0_conv_in['out_b']}

def reference(x, L0_conv_ln_gamma, L0_conv_ln_beta, L0_conv_mlp_w1, L0_conv_mlp_b1, L0_conv_mlp_w2, L0_conv_mlp_b2, L0_conv_in_w, L0_conv_in_b, L0_conv_gru_wih_f, L0_conv_gru_whh_f, L0_conv_gru_bih_f, L0_conv_gru_bhh_f, L0_conv_gru_wih_b, L0_conv_gru_whh_b, L0_conv_gru_bih_b, L0_conv_gru_bhh_b, L0_conv_out_w, L0_conv_out_b):
    import jax
    import jax.numpy as jnp

    def _L0_conv_ref(x, ln_gamma, ln_beta, mlp_w1, mlp_b1, mlp_w2, mlp_b2, in_w, in_b, gru_wih_f, gru_whh_f, gru_bih_f, gru_bhh_f, gru_wih_b, gru_whh_b, gru_bih_b, gru_bhh_b, out_w, out_b):
        import jax, jax.numpy as jnp
        import numpy as np
        B, H, W, DIM = (16, 32, 32, 128)
        EXPAND = 2
        D_INNER = DIM * EXPAND
        HID = D_INNER // 2

        def _resize_linear_axis(x, out_size, axis):
            in_size = x.shape[axis]
            scale = in_size / out_size
            src = (jnp.arange(out_size, dtype=jnp.float32) + 0.5) * scale - 0.5
            src = jnp.clip(src, 0.0, in_size - 1)
            i0 = jnp.floor(src).astype(jnp.int32)
            i1 = jnp.minimum(i0 + 1, in_size - 1)
            w = src - i0.astype(jnp.float32)
            x0 = jnp.take(x, i0, axis=axis)
            x1 = jnp.take(x, i1, axis=axis)
            shape = [1] * x.ndim
            shape[axis] = out_size
            w = w.reshape(shape)
            return x0 * (1.0 - w) + x1 * w

        def _avgpool3_mean(g):
            s = jax.lax.reduce_window(g, 0.0, jax.lax.add, (1, 1, 3, 3), (1, 1, 1, 1), [(0, 0), (0, 0), (1, 1), (1, 1)])
            return (s / 9.0).mean(axis=(2, 3))

        def _gru_dir(xp, whh, bhh, reverse):
            hid = whh.shape[1]
            h0 = jnp.zeros((xp.shape[0], hid), xp.dtype)

            def step(h, xt):
                gh = h @ whh.T + bhh
                xr, xz, xn = jnp.split(xt, 3, axis=-1)
                hr, hz, hn = jnp.split(gh, 3, axis=-1)
                r = jax.nn.sigmoid(xr + hr)
                z = jax.nn.sigmoid(xz + hz)
                n = jnp.tanh(xn + r * hn)
                h_new = (1.0 - z) * n + z * h
                return (h_new, h_new)
            _, ys = jax.lax.scan(step, h0, jnp.swapaxes(xp, 0, 1), reverse=reverse)
            return jnp.swapaxes(ys, 0, 1)

        def _forward(x, ln_gamma, ln_beta, mlp_w1, mlp_b1, mlp_w2, mlp_b2, in_w, in_b, gru_wih_f, gru_whh_f, gru_bih_f, gru_bhh_f, gru_wih_b, gru_whh_b, gru_bih_b, gru_bhh_b, out_w, out_b):
            Bx, Hx, Wx, C = x.shape
            mu = x.mean(-1, keepdims=True)
            var = ((x - mu) ** 2).mean(-1, keepdims=True)
            xn = (x - mu) / jnp.sqrt(var + 1e-05) * ln_gamma + ln_beta
            gray = xn.mean(-1)[:, None]
            gp = jnp.pad(gray, ((0, 0), (0, 0), (1, 1), (1, 1)), mode='reflect')
            grad_h = jnp.abs(gp[:, :, :, 2:] - gp[:, :, :, :-2])
            grad_v = jnp.abs(gp[:, :, 2:, :] - gp[:, :, :-2, :])
            grad_h = _resize_linear_axis(grad_h, Hx, axis=2)
            grad_v = _resize_linear_axis(grad_v, Wx, axis=3)
            grad_d = (grad_h + grad_v) * 0.5
            grad_a = jnp.abs(grad_h - grad_v)
            scores = jnp.concatenate([_avgpool3_mean(g) for g in (grad_h, grad_v, grad_d, grad_a)], axis=1)
            h1 = jax.nn.relu(scores @ mlp_w1.T + mlp_b1)
            logits = h1 @ mlp_w2.T + mlp_b2
            probs = jax.nn.softmax(logits, axis=-1)
            idx = jnp.argmax(probs, axis=-1)
            seq_h = xn.reshape(Bx, Hx * Wx, C)
            seq_v = jnp.swapaxes(xn, 1, 2).reshape(Bx, Hx * Wx, C)
            seq = jnp.where((idx == 1)[:, None, None], seq_v, seq_h)
            z = seq @ in_w.T + in_b
            yf = _gru_dir(z @ gru_wih_f.T + gru_bih_f, gru_whh_f, gru_bhh_f, False)
            yb = _gru_dir(z @ gru_wih_b.T + gru_bih_b, gru_whh_b, gru_bhh_b, True)
            y = jnp.concatenate([yf, yb], axis=-1) @ out_w.T + out_b
            return x + y.reshape(Bx, Hx, Wx, C)
        return _forward(x, ln_gamma, ln_beta, mlp_w1, mlp_b1, mlp_w2, mlp_b2, in_w, in_b, gru_wih_f, gru_whh_f, gru_bih_f, gru_bhh_f, gru_wih_b, gru_whh_b, gru_bih_b, gru_bhh_b, out_w, out_b)

    def _gn(v, G=32, eps=1e-05):
        B_, H_, W_, C_ = v.shape
        g = v.reshape(B_, H_, W_, G, C_ // G)
        m = jnp.mean(g, axis=(1, 2, 4), keepdims=True)
        s = jnp.var(g, axis=(1, 2, 4), keepdims=True)
        return ((g - m) / jnp.sqrt(s + eps)).reshape(v.shape)

    def _ln_c(v, eps=1e-06):
        m = jnp.mean(v, axis=-1, keepdims=True)
        s = jnp.var(v, axis=-1, keepdims=True)
        return (v - m) / jnp.sqrt(s + eps)

    def _ln_t(v, eps=1e-05):
        m = jnp.mean(v, axis=-1, keepdims=True)
        s = jnp.var(v, axis=-1, keepdims=True)
        return (v - m) / jnp.sqrt(s + eps)

    def _to_tokens(v):
        B_, H_, W_, C_ = v.shape
        return v.reshape(B_, H_ * W_, C_)

    def _from_tokens(t, like):
        return t.reshape(like.shape)
    x = _L0_conv_ref(x, L0_conv_ln_gamma, L0_conv_ln_beta, L0_conv_mlp_w1, L0_conv_mlp_b1, L0_conv_mlp_w2, L0_conv_mlp_b2, L0_conv_in_w, L0_conv_in_b, L0_conv_gru_wih_f, L0_conv_gru_whh_f, L0_conv_gru_bih_f, L0_conv_gru_bhh_f, L0_conv_gru_wih_b, L0_conv_gru_whh_b, L0_conv_gru_bih_b, L0_conv_gru_bhh_b, L0_conv_out_w, L0_conv_out_b)
    return x

_drawn_inputs = setup_inputs


def setup_inputs(seed=0):
    import zlib

    import numpy as np

    out = dict(_drawn_inputs(seed))
    spreads = {'L0_conv_ln_gamma': (1.0, 0.2),
     'L0_conv_ln_beta': (0.0, 0.271),
     'L0_conv_mlp_b1': (0.0, 0.1),
     'L0_conv_mlp_b2': (0.0, 0.1),
     'L0_conv_in_b': (0.0, 0.1),
     'L0_conv_gru_bih_f': (0.0, 0.1),
     'L0_conv_gru_bhh_f': (0.0, 0.287),
     'L0_conv_gru_bih_b': (0.0, 0.1),
     'L0_conv_gru_bhh_b': (0.0, 0.282),
     'L0_conv_out_b': (0.0, 0.1)}
    factors = {}
    for name, (base, spread) in spreads.items():
        noise = np.random.default_rng([zlib.crc32(name.encode()), seed]).standard_normal(out[name].shape)
        drawn = base * np.exp(spread * noise) if base else spread * noise
        out[name] = jnp.asarray(drawn.astype(out[name].dtype))
    for name, factor in factors.items():
        out[name] = (out[name] * factor).astype(out[name].dtype)
    return out
```

```python
from contextlib import ExitStack

import concourse.bass as bass
from concourse import mybir

P = 128
B, H, WD, C = 16, 32, 32, 128
L = H * WD
DI = 2 * C
HID = 128
TB = 8
NBLK = L // TB
RING = 2 * TB
COLS = 2 * B
TPP = L // P
EPS = 1e-5

F32 = mybir.dt.float32
BF16 = mybir.dt.bfloat16
I32 = mybir.dt.int32
ALU = mybir.AluOpType
ACT = mybir.ActivationFunctionType
AX = mybir.AxisListType.X
G_R, G_Z, G_N, G_HN = range(4)

C_IDENT, C_SLIDE, C_DIFF, C_RESIZE, C_POOLH = 0, 128, 191, 223, 255
C_WLO = 271
C_WHI = C_WLO + WD
C_POOLW = C_WHI + WD
C_ONES = C_POOLW + WD
C_IND = C_ONES + P
C_END = C_IND + 2 * P


def shape_constants():
    import numpy as np

    t = np.zeros((P, C_END), np.float32)
    t[:, C_IDENT:C_IDENT + P] = np.eye(P)
    t[:, C_SLIDE + H - 1] = 1.0 / C
    for i in range(1, H - 1):
        t[i + 1, C_DIFF + i] += 1.0
        t[i - 1, C_DIFF + i] -= 1.0
    for i in range(H):
        src = min(max((i + 0.5) * (H + 2) / H - 0.5, 0.0), H + 1)
        lo = int(np.floor(src))
        w = src - lo
        for k, v in ((lo, 1.0 - w), (min(lo + 1, H + 1), w)):
            row = k - 1
            row = -row if row < 0 else (2 * (H - 1) - row if row > H - 1 else row)
            t[row, C_RESIZE + i] += v
        t[:, C_WLO + i] = 1.0 - w
        t[:, C_WHI + i] = w
        edge = 2.0 if i in (0, H - 1) else 3.0
        for k in range(4):
            t[i, C_POOLH + 4 * k + k] = edge / (9.0 * H * WD)
        t[:, C_POOLW + i] = edge
    t[:, C_ONES:C_ONES + P] = 1.0
    ind = t[:, C_IND:C_IND + 2 * P].reshape(P, TB, 2, B)
    for part in range(3):
        for d in range(2):
            ind[2 * part + d, :, d, :] = 1.0
    t[:, C_IND:C_IND + 2 * P] = ind.reshape(P, 2 * P)
    return t


def build(nc, x, gamma, beta, w1t, b1, w2t, b2, in_w, in_b, wiht, whht, bih, bhh, outwt, out_b, consts, out):
    ctx = ExitStack()

    def sb(name, shape, dt=F32):
        return ctx.enter_context(nc.sbuf_tensor(name, shape, dt))

    def sem(name):
        return ctx.enter_context(nc.semaphore(name))

    seq = sb("seq", [P, L, B])
    big = sb("big", [P, L * B])
    seq_v = big[:, :].rearrange("c (t b) -> c t b", b=B)
    tiles = big[:, :].rearrange("p (k c) -> p k c", c=C)
    xin = sb("xin", [P, 2, TPP, C])
    xhat = sb("xhat", [P, 2, TPP, C])
    stats = sb("stats", [P, 2, TPP, 6])
    moments = sb("moments", [P, 2, TPP, 2])
    std = sb("std", [P, 2, TPP])
    rstd = sb("rstd", [P, 2, TPP])
    shift = sb("shift", [P, 2, TPP])
    gb = sb("gb", [P, 2])
    eps = sb("eps", [P, 1])
    con = sb("con", [P, C_END])
    ind = sb("ind", [6, 2 * P], BF16)
    ones_bf = sb("ones_bf", [1, P], BF16)
    inw = sb("inw", [P, DI // P, C])
    inb = sb("inb", [P, DI // P])
    wih = sb("wih", [P, 2, DI // P, 3 * HID])
    whh = sb("whh", [P, 2, 3 * HID])
    wsplit = sb("wsplit", [P, 3, 2, 3 * HID], BF16)
    wcomb = sb("wcomb", [P, 2, 3 * HID])
    outw = sb("outw", [P, 2, C])
    brow = sb("brow", [1, 3, 2, 4 * HID])
    bsplit = sb("bsplit", [1, 3, 2 * 4 * HID + C], BF16)
    bias6 = sb("bias6", [6, 4 * HID], BF16)
    obrow = sb("obrow", [1, 2, C])
    obias = sb("obias", [3, C], BF16)
    ones3 = sb("ones3", [3, P], BF16)
    mlp1 = sb("mlp1", [4, 32])
    mlpb1 = sb("mlpb1", [32, 1])
    mlp2 = sb("mlp2", [32, 4])
    mlpb2 = sb("mlpb2", [B, 4])
    g4 = xin[0:H].rearrange("h q j c -> h (q j c)").rearrange("h (k w b) -> h k w b", k=4, b=B)
    spare = xhat[0:H].rearrange("h q j c -> h (q j c)").rearrange("h (w b) -> h w b", b=B)
    gray, gv, gh = spare[:, 0:WD + 2], spare[:, WD + 2:2 * WD + 4], spare[:, 2 * WD + 4:3 * WD + 4]
    gt = sb("gt", [H, WD, B])
    pooled = sb("pooled", [H, 4, B])
    scores = sb("scores", [4, B])
    hid1 = sb("hid1", [32, B])
    lg = sb("lg", [B, 16])
    diag = sb("diag", [B, B])
    mask = sb("mask", [P, B], I32)
    rev = sb("rev", [P, 2, TB, B])
    hist = sb("hist", [P, 2, 2, B, TB])
    state = sb("state", [P, RING, 3 * COLS])
    resid = sb("resid", [P, 2, COLS])
    low = sb("low", [P, 2, COLS], BF16)
    rpair = sb("rpair", [P, 2, 2 * COLS])
    ztrip = sb("ztrip", [P, 2, 3 * COLS])

    bank = [ctx.enter_context(nc.psum_tensor(f"bank{i}", [P, 512], F32)) for i in range(8)]
    R, Z, NX, Y = bank[0:2], bank[2:4], bank[4:6], bank[6]
    cand = bank[7]

    w_in = sem("w_in")
    x_in0 = sem("x_in0")
    x_in1 = sem("x_in1")
    stats_set = sem("stats_set")
    moments_set = sem("moments_set")
    std_set = sem("std_set")
    rstd_set = sem("rstd_set")
    shift_set = sem("shift_set")
    xhat_set = sem("xhat_set")
    xT_set = sem("xT_set")
    seq_set = sem("seq_set")
    seqv_set = sem("seqv_set")
    w_mm = sem("w_mm")
    link_v = sem("link_v")
    bias_set = sem("bias_set")
    bias_rows = sem("bias_rows")
    cast_set = sem("cast_set")
    weights_set = sem("weights_set")
    gray_mm = sem("gray_mm")
    gray_set = sem("gray_set")
    diff_mm = sem("diff_mm")
    gradh_set = sem("gradh_set")
    rows_mm = sem("rows_mm")
    gradv_set = sem("gradv_set")
    cols_set = sem("cols_set")
    pooled_set = sem("pooled_set")
    scores_mm = sem("scores_mm")
    scores_set = sem("scores_set")
    hid_mm = sem("hid_mm")
    hid_set = sem("hid_set")
    logits_mm = sem("logits_mm")
    logits_set = sem("logits_set")
    exp_set = sem("exp_set")
    diag_set = sem("diag_set")
    mask_mm = sem("mask_mm")
    select_done = sem("select_done")
    init_done = sem("init_done")
    reset_pre = sem("reset_pre")
    hn_ready = sem("hn_ready")
    update_pre = sem("update_pre")
    reset_ready = sem("reset_ready")
    update_ready = sem("update_ready")
    cand_pre = sem("cand_pre")
    cand_ready = sem("cand_ready")
    state_ready = sem("state_ready")
    resid_ready = sem("resid_ready")
    low_ready = sem("low_ready")
    neg_ready = sem("neg_ready")
    hist_ready = sem("hist_ready")
    rev_ready = sem("rev_ready")
    images_counted = sem("images_counted")
    blocks_counted = sem("blocks_counted")
    y_ready = sem("y_ready")
    y_used = sem("y_used")
    tile_in0 = sem("tile_in0")
    tile_in1 = sem("tile_in1")
    out_done = sem("out_done")
    x_in = (x_in0, x_in1)
    tile_in = (tile_in0, tile_in1)

    x_tok = x.rearrange("b h w c -> b (h w) c")
    out_tok = out.rearrange("b h w c -> b (h w) c")
    x_part = x_tok.rearrange("b (p j) c -> b p (j c)", j=TPP)

    block = ctx.enter_context(nc.Block())

    @block.sync
    def _(sp):
        def load_image(b, q, wait):
            if wait is not None:
                sp.wait_ge(xhat_set, wait)
            sp.dma_start(xin[:, q].rearrange("p j c -> p (j c)"),
                         x_part[bass.ds(b, 1)].rearrange("a p n -> (a p) n") if not isinstance(b, int) else x_part[b]
                         ).then_inc(x_in[q], 16)

        load_image(0, 0, None)
        load_image(1, 1, None)
        with sp.Fori(1, B // 2) as i:
            for q in range(2):
                load_image(i * 2 + q, q, i * 2 + (q - 1))
        sp.wait_ge(select_done, 1)

        def tile_rows(t, k):
            return t[:, bass.ds(k * TB, TB), :]

        def load_tiles(k, q, wait):
            if wait is not None:
                sp.wait_ge(y_used, wait)
            for kk in (k, k * -1 + (NBLK - 1)):
                sp.dma_start(tiles[:, bass.ds(kk, 1), :].rearrange("p a c -> p (a c)"),
                             tile_rows(x_tok, kk)).then_inc(tile_in[q], 16)

        load_tiles(0, 0, None)
        load_tiles(1, 1, None)
        with sp.Fori(1, NBLK // 4) as i:
            for q in range(2):
                load_tiles(i * 2 + q, q, i * 4 + (2 * q - 2))
        with sp.Fori(NBLK // 4, NBLK // 2) as i:
            for q in range(2):
                for d in range(2):
                    k = i * 2 + q
                    kk = k if d == 0 else k * -1 + (NBLK - 1)
                    sp.wait_ge(y_used, i * 4 + (2 * q + d + 1))
                    sp.dma_start(tile_rows(out_tok, kk),
                                 tiles[:, bass.ds(kk, 1), :].rearrange("p a c -> p (a c)")).then_inc(out_done, 16)
        sp.wait_ge(out_done, 16 * NBLK)

    N_PARAM = 20
    EARLY_N = 3
    N_INIT = 7

    @block.gpsimd
    def _(g):
        n = 0
        for dst, src in (
            (con[:, :], consts), (gb[:, 0:1], gamma),
            (gb[:, 1:2], beta),
            (inw[:, :, :], in_w.rearrange("(k p) c -> p k c", p=P)),
            (inb[:, :], in_b),
            (wih[:, 0], wiht[0].rearrange("(k p) m -> p k m", p=P)),
            (wih[:, 1], wiht[1].rearrange("(k p) m -> p k m", p=P)),
            (whh[:, 0], whht[0]), (whh[:, 1], whht[1]),
            (outw[:, 0], outwt[0:HID]), (outw[:, 1], outwt[HID:2 * HID]),
            (mlp1[:, :], w1t), (mlpb1[:, :], b1), (mlp2[:, :], w2t),
            (mlpb2[:, :], b2.to_broadcast((B, 4))),
            (brow[0:1, 1, 0, 0:3 * HID], bih[0]), (brow[0:1, 1, 1, 0:3 * HID], bih[1]),
            (brow[0:1, 2, 0, 0:3 * HID], bhh[0]), (brow[0:1, 2, 1, 0:3 * HID], bhh[1]),
            (obrow[0:1, 0, :], out_b),
        ):
            g.dma_start(dst, src).then_inc(w_in, 16)
            n += 1
        assert n == N_PARAM
        g.memset(rpair[:, :, :], 0.0).then_inc(init_done, 1)
        g.memset(ztrip[:, :, :], 0.0).then_inc(init_done, 1)
        g.memset(state[:, :, :], 0.0).then_inc(init_done, 1)
        g.memset(resid[:, :, :], 0.0).then_inc(init_done, 1)
        g.memset(low[:, :, :], 0.0).then_inc(init_done, 1)
        g.wait_ge(init_done, 5)
        for q in range(2):
            g.memset(ztrip[:, q, :].rearrange("p (n e) -> p n e", e=3)[:, :, 1], 1.0).then_inc(init_done, 1)
        g.wait_ge(bias_set, 1)
        for k in range(3):
            for d in range(2):
                g.dma_start(bias6[2 * k + d:2 * k + d + 1, :],
                            bsplit[0:1, k, d * 4 * HID:(d + 1) * 4 * HID]).then_inc(bias_rows, 16)
            g.dma_start(obias[k:k + 1, :], bsplit[0:1, k, 8 * HID:8 * HID + C]).then_inc(bias_rows, 16)

        def reorder(k, q, wait):
            g.wait_ge(state_ready, (k + 1) * TB)
            if wait:
                g.wait_ge(y_ready, k - 1)
            g.sem_inc(blocks_counted, 1)
            for d in range(2):
                h = state[:, q * TB:(q + 1) * TB, :].rearrange("p s (d b k) -> p s d b k", d=2, k=3)[:, :, d, :, 2]
                if d == 0:
                    ins = g.tensor_copy(hist[:, q, d], h.rearrange("p s b -> p b s"))
                else:
                    for s in range(TB):
                        ins = g.tensor_copy(hist[:, q, d, :, TB - 1 - s], h[:, s, :])
            ins.then_inc(hist_ready, 1)

        def reverse(k, q):
            for s in range(TB):
                ins = g.tensor_copy(rev[:, q, s, :], seq[:, bass.ds(k * -TB + (L - 1 - s), 1), :].rearrange("c a b -> c (a b)"))
            ins.then_inc(rev_ready, 1)

        g.wait_ge(select_done, 1)
        for q in range(2):
            reverse(q, q)
        for q in range(2):
            reorder(q, q, False)
            reverse(q + 2, q)
        with g.Fori(1, NBLK // 2 - 1) as i:
            for q in range(2):
                reorder(i * 2 + q, q, True)
                reverse(i * 2 + (q + 2), q)
        for q in range(2):
            reorder(NBLK - 2 + q, q, True)

    @block.scalar
    def _(act):
        def normalise(q, turn, first):
            act.wait_ge(moments_set, turn)
            act.activation(std[:, q, :], moments[:, q, :, 1], ACT.Sqrt, bias=eps[:, 0:1]).then_inc(std_set, 1)
            act.wait_ge(shift_set, turn)
            if not first:
                act.wait_ge(xT_set, turn * 2 - 4)
            for j in range(TPP):
                ins = act.activation(xhat[:, q, j, :], xin[:, q, j, :], ACT.Identity,
                                     bias=shift[:, q, j:j + 1], scale=rstd[:, q, j:j + 1])
            ins.then_inc(xhat_set, 1)

        def evacuate(b, q, turn):
            for half in range(2):
                act.wait_ge(xT_set, turn * 2 + (half - 1))
                dst = seq[:, :, :].rearrange("c (p j) b -> c j p b", j=TPP)[:, 4 * half:4 * half + 4, :, bass.ds(b, 1)]
                act.activation(dst.rearrange("c j p b -> c j (p b)"),
                               bank[2 * q + half][:, :].rearrange("c (j p) -> c j p", j=4), ACT.Identity,
                               bias=gb[:, 1:2], scale=gb[:, 0:1]).then_inc(seq_set, 1)

        act.wait_ge(cast_set, 1)
        normalise(0, 1, True)
        normalise(1, 2, True)
        act.wait_ge(w_in, 16 * N_PARAM)
        evacuate(0, 0, 1)
        with act.Fori(1, B // 2) as i:
            for q in range(2):
                normalise(q, i * 2 + (q + 1), False)
                evacuate(i * 2 + (q - 1), 1 - q, i * 2 + q)
        evacuate(B - 1, 1, B)

        act.wait_ge(logits_set, 1)
        act.activation(lg[:, 4:8], lg[:, 0:4], ACT.Exp, bias=lg[:, 12:13]).then_inc(exp_set, 1)

        act.wait_ge(init_done, N_INIT)

        with act.Fori(0, L // RING) as i:
            for r in range(RING):
                q, s, e = r // TB, r % TB, r % 2
                turn = i * RING + (r + 1)
                act.wait_ge(reset_pre, turn)
                act.activation(rpair[:, e, :].rearrange("p (d n k) -> p d n k", d=2, k=2)[:, :, :, 1],
                               R[q][:, s * COLS:(s + 1) * COLS].rearrange("p (d b) -> p d b", d=2), ACT.Sigmoid).then_inc(reset_ready, 1)
                act.wait_ge(update_pre, turn)
                act.activation(ztrip[:, e, :].rearrange("p (d n k) -> p d n k", d=2, k=3)[:, :, :, 2],
                               Z[q][:, s * COLS:(s + 1) * COLS].rearrange("p (d b) -> p d b", d=2), ACT.Sigmoid, scale=-1.0).then_inc(update_ready, 1)
                act.wait_ge(cand_pre, turn)
                act.activation(state[:, (r - 1) % RING, :].rearrange("p (n k) -> p n k", k=3)[:, :, 0],
                               cand[:, e * 2 * COLS:(e + 1) * 2 * COLS].rearrange("p (n k) -> p n k", k=2)[:, :, 1],
                               ACT.Tanh).then_inc(cand_ready, 1)

    @block.tensor
    def _(pe):
        identity = con[:, C_IDENT:C_IDENT + P]
        pe.wait_ge(w_in, 16 * N_PARAM)
        for d in range(2):
            for k in range(DI // P):
                nc.tensor.matmul(bank[4 + d][:, 0:3 * HID], inw[:, k, :], wih[:, d, k, :],
                                 start=(k == 0), stop=(k == DI // P - 1))
            for k in range(DI // P):
                ins = nc.tensor.matmul(bank[6 + d][0:1, 0:3 * HID], inb[:, k:k + 1], wih[:, d, k, :],
                                       start=(k == 0), stop=(k == DI // P - 1))
        ins.then_inc(w_mm, 1)

        def transposes(q, turn, first):
            pe.wait_ge(xhat_set, turn)
            for half in range(2):
                if not first:
                    pe.wait_ge(seqv_set, turn * 2 + (half - 5))
                for j in range(4):
                    ins = nc.tensor.transpose(bank[2 * q + half][:, j * P:(j + 1) * P],
                                              xhat[:, q, 4 * half + j, :], identity)
                ins.then_inc(xT_set, 1)

        transposes(0, 1, True)
        transposes(1, 2, True)
        with pe.Fori(1, B // 2) as i:
            for q in range(2):
                transposes(q, i * 2 + (q + 1), False)

        pe.wait_ge(seq_set, 2 * B)
        pe.wait_ge(weights_set, 2)
        for h in range(H):
            ins = nc.tensor.matmul(bank[4][0:H, :], con[:, C_SLIDE + H - 1 - h:C_SLIDE + 2 * H - 1 - h],
                                   seq[:, h * WD:(h + 1) * WD, :].rearrange("c t b -> c (t b)"),
                                   start=(h == 0), stop=(h == H - 1))
        ins.then_inc(gray_mm, 1)
        pe.wait_ge(gray_set, 1)
        nc.tensor.matmul(bank[5][0:H, :], con[0:H, C_DIFF:C_DIFF + H],
                         gray[:, 1:WD + 1, :].rearrange("h w b -> h (w b)"), start=True, stop=True).then_inc(diff_mm, 1)
        pe.wait_ge(gradh_set, 1)
        nc.tensor.matmul(bank[4][0:H, :], con[0:H, C_RESIZE:C_RESIZE + H],
                         gh[:, :, :].rearrange("h w b -> h (w b)"), start=True, stop=True).then_inc(rows_mm, 1)
        pe.wait_ge(pooled_set, 1)
        for k in range(4):
            ins = nc.tensor.matmul(bank[5][0:4, 0:B], con[0:H, C_POOLH + 4 * k:C_POOLH + 4 * k + 4],
                                   pooled[:, k, :], start=(k == 0), stop=(k == 3))
        ins.then_inc(scores_mm, 1)
        pe.wait_ge(scores_set, 1)
        nc.tensor.matmul(bank[4][0:32, 0:B], mlp1[:, :], scores[:, :], start=True, stop=True).then_inc(hid_mm, 1)
        pe.wait_ge(hid_set, 1)
        nc.tensor.matmul(bank[5][0:B, 0:4], hid1[:, :], mlp2[:, :], start=True, stop=True).then_inc(logits_mm, 1)
        pe.wait_ge(diag_set, 1)
        nc.tensor.matmul(bank[4][:, 0:B], con[0:B, C_ONES:C_ONES + P], diag[:, :], start=True, stop=True).then_inc(mask_mm, 1)

        def mm(o, w, m, start=False):
            return nc.tensor.matmul(o, w, m, start=start, stop=True, skip_group_check=True)

        def nx(q):
            return NX[q][:, :].rearrange("p (s d b k) -> p s d b k", s=TB, d=2, k=2)

        def gate(banks, q):
            return banks[q][:, 0:TB * COLS].rearrange("p (s d b) -> p s d b", s=TB, d=2)

        def fill_bias(q, which):
            if which in (G_R, G_Z):
                bk = (R if which == G_R else Z)[q]
                return mm(bk[:, 0:2 * TB * B], bias6[:, which * HID:(which + 1) * HID],
                          ind[:, :], start=True)
            k = 0 if which == G_HN else 1
            return mm(NX[q][:, k::2], bias6[:, which * HID:(which + 1) * HID],
                      ind[:, :], start=(which == G_HN))

        def fill_input(q, kblk, g, d):
            src = seq[:, bass.ds(kblk * TB, TB), :] if d == 0 else rev[:, q]
            w = wcomb[:, d, g * HID:(g + 1) * HID]
            if g == G_N:
                return mm(nx(q)[:, :, d, :, 1], w, src)
            return mm(gate(R if g == G_R else Z, q)[:, :, d, :], w, src)

        FILL = [[("b", G_R), ("b", G_Z), ("b", G_HN), ("b", G_N)], [(G_R, 0)], [(G_Z, 0)], [(G_N, 0)],
                [(G_R, 1)], [(G_Z, 1)], [(G_N, 1)], []]
        FIRST_BACKWARD = 4

        def fill(q, kblk, items, rev_turn=None):
            if rev_turn is not None:
                pe.wait_ge(rev_ready, rev_turn)
            for it in items:
                if it[0] == "b":
                    fill_bias(q, it[1])
                else:
                    fill_input(q, kblk, *it)

        def project(q, d):
            return mm(Y[:, d * C:(d + 1) * C], hist[:, q, d].rearrange("p b s -> p (b s)"), outw[:, d, :],
                      start=(d == 0))

        def project_forward(q):
            project(q, 0)
            return mm(Y[:, 0:C], ones3[:, :], obias[:, :])

        def step(base, r):
            q, s, e = r // TB, r % TB, r % 2
            prev = (r - 1) % RING
            h0 = state[:, prev, :].bitcast(BF16).rearrange("p (d b k) -> p d b k", d=2, k=6)[:, :, :, 5]
            h1 = resid[:, 1 - e, :].bitcast(BF16).rearrange("p (d b k) -> p d b k", d=2, k=2)[:, :, :, 1]
            h2 = low[:, 1 - e, :].rearrange("p (d b) -> p d b", d=2)

            def dst(g, d):
                if g == G_N:
                    return nx(q)[:, s, d, :, 0]
                return gate(R if g == G_R else Z, q)[:, s, d, :]

            def run(g, d, k, hp):
                return mm(dst(g, d), wsplit[:, k, d, g * HID:(g + 1) * HID], hp[:, d, :])

            step0 = isinstance(base, int) and base + r == 0
            if not step0:
                pe.wait_ge(state_ready, base + r)
            for g, ks in ((G_R, 3), (G_N, EARLY_N)):
                for d in range(2):
                    for k in range(ks):
                        run(g, d, k, h0)
            if not step0:
                pe.wait_ge(resid_ready, base + r)
            for d in range(2):
                for k in range(2):
                    run(G_R, d, k, h1)
            if not step0:
                pe.wait_ge(low_ready, base + r)
            for d in range(2):
                ins = run(G_R, d, 0, h2)
            ins.then_inc(reset_pre, 1)
            for d in range(2):
                for k in range(EARLY_N, 3):
                    run(G_N, d, k, h0)
                for k in range(2):
                    run(G_N, d, k, h1)
                ins = run(G_N, d, 0, h2)
            ins.then_inc(hn_ready, 1)
            for d in range(2):
                for k in range(3):
                    run(G_Z, d, k, h0)
                for k in (0, 1):
                    run(G_Z, d, k, h1)
                ins = run(G_Z, d, 0, h2)
            ins.then_inc(update_pre, 1)

        def body(base, kblk, first=False, last=False):
            for r in range(RING):
                q, s = r // TB, r % TB
                step(base, r)
                if not (last and q == 1):
                    fill(1 - q, kblk + (q + 1), FILL[s], kblk + (q + 2) if s == FIRST_BACKWARD else None)
                if s == TB - 1 and not (first and q == 0):
                    if not (first and q == 1):
                        pe.wait_ge(y_used, (kblk + (q - 1)) * 2)
                    pe.wait_ge(hist_ready, kblk + q)
                    project_forward(1 - q)
                if s == 0 and not (first and q == 0) and not (first and q == 1):
                    project(q, 1).then_inc(y_ready, 1)

        pe.wait_ge(bias_rows, 16 * 9)
        pe.wait_ge(cast_set, 2)
        pe.wait_ge(weights_set, 2)
        pe.wait_ge(select_done, 1)
        pe.wait_ge(init_done, N_INIT)
        for items in FILL:
            fill(0, 0, items, 1)
        body(0, 0, first=True)
        with pe.Fori(1, L // RING - 1) as i:
            body(i * RING, i * 2)
        body(L - RING, NBLK - 2, last=True)
        project(0, 1).then_inc(y_ready, 1)
        pe.wait_ge(y_used, 2 * (NBLK - 1))
        pe.wait_ge(hist_ready, NBLK)
        project_forward(1)
        project(1, 1).then_inc(y_ready, 1)

    @block.vector
    def _(dve):
        v = nc.vector
        links = [0]

        def link(ins):
            links[0] += 1
            ins.then_inc(link_v, 1)
            dve.wait_ge(link_v, links[0])

        link(v.memset(ones3[:, :], 1.0))
        v.memset(eps[:, :], EPS).then_inc(cast_set, 1)

        def statistics(q, turn, landed, first):
            dve.wait_ge(x_in[q], landed)
            if not first:
                dve.wait_ge(std_set, turn - 2)
                dve.wait_ge(xhat_set, turn - 2)
            for j in range(TPP):
                ins = v.bn_stats(out=stats[:, q, j, :], in_=xin[:, q, j, :])
            ins.then_inc(stats_set, 1)
            dve.wait_ge(stats_set, turn)
            dve.sem_inc(images_counted, 1)
            for j in range(TPP):
                ins = v.bn_aggr(out=moments[:, q, j, :], in_=stats[:, q, j, :])
            ins.then_inc(moments_set, 1)
            dve.wait_ge(std_set, turn)
            v.reciprocal(rstd[:, q, :], std[:, q, :]).then_inc(rstd_set, 1)
            dve.wait_ge(rstd_set, turn)
            dve.wait_ge(moments_set, turn)
            v.scalar_tensor_tensor(out=shift[:, q, :], in0=moments[:, q, :, 0], scalar=-1.0, in1=rstd[:, q, :],
                                   op0=ALU.mult, op1=ALU.mult).then_inc(shift_set, 1)

        def evacuate_columns(b, q, turn):
            hp = WD // TPP
            for half in range(2):
                dve.wait_ge(seq_set, turn * 2 + (half - 1))
                dst = seq_v.rearrange("c (m j h) b -> c j h m b", m=hp, j=TPP)[
                    :, 4 * half:4 * half + 4, :, :, bass.ds(b, 1)].rearrange("c j h m b -> c j h (m b)")
                v.tensor_scalar(dst, bank[2 * q + half][:, :].rearrange("c (j h m) -> c j h m", j=4, m=hp),
                                gb[:, 0:1], gb[:, 1:2], ALU.mult, ALU.add).then_inc(seqv_set, 1)

        statistics(0, 1, 16, True)
        statistics(1, 2, 16, True)
        dve.wait_ge(w_in, 16 * N_PARAM)
        evacuate_columns(0, 0, 1)
        with dve.Fori(1, B // 2) as i:
            for q in range(2):
                statistics(q, i * 2 + (q + 1), i * 16 + 16, False)
                evacuate_columns(i * 2 + (q - 1), 1 - q, i * 2 + q)
        evacuate_columns(B - 1, 1, B)

        w_all = whh[:, :, :].rearrange("p d n -> p (d n)")
        parts = [wsplit[:, k].rearrange("p d n -> p (d n)") for k in range(3)]
        link(v.tensor_copy(parts[0], w_all))
        link(v.tensor_tensor(w_all, w_all, parts[0], ALU.subtract))
        link(v.tensor_copy(parts[1], w_all))
        link(v.tensor_tensor(w_all, w_all, parts[1], ALU.subtract))
        v.tensor_copy(parts[2], w_all).then_inc(weights_set, 1)
        dve.wait_ge(w_mm, 1)
        for d in range(2):
            ins = v.tensor_copy(wcomb[:, d, :], bank[4 + d][:, 0:3 * HID])
        ins.then_inc(weights_set, 1)
        for d in range(2):
            link(v.tensor_tensor(brow[0:1, 0, d, 0:3 * HID], bank[6 + d][0:1, 0:3 * HID],
                                 brow[0:1, 1, d, 0:3 * HID], ALU.add))
            link(v.tensor_tensor(brow[0:1, 0, d, 0:2 * HID], brow[0:1, 0, d, 0:2 * HID],
                                 brow[0:1, 2, d, 0:2 * HID], ALU.add))
            link(v.tensor_copy(brow[0:1, 0, d, 3 * HID:4 * HID], brow[0:1, 2, d, 2 * HID:3 * HID]))
        for src, at in ((brow[0:1, 0, :, :].rearrange("a d n -> a (d n)"), 0), (obrow[0:1, 0, :], 8 * HID)):
            n = src.shape[-1]
            for k in range(3):
                link(v.tensor_copy(bsplit[0:1, k, at:at + n], src))
                if k < 2:
                    link(v.tensor_tensor(src, src, bsplit[0:1, k, at:at + n], ALU.subtract))
        v.tensor_copy(ind[:, :], con[0:6, C_IND:C_IND + 2 * P]).then_inc(bias_set, 1)
        dve.wait_ge(bias_set, 1)
        v.tensor_copy(ones_bf[:, :], con[0:1, C_ONES:C_ONES + P]).then_inc(cast_set, 1)

        def absolute(dst, src):
            return v.scalar_tensor_tensor(out=dst, in0=src, scalar=-1.0, in1=src, op0=ALU.mult, op1=ALU.max)

        dve.wait_ge(gray_mm, 1)
        link(v.tensor_copy(gray[:, 1:WD + 1, :].rearrange("h w b -> h (w b)"), bank[4][0:H, :]))
        v.tensor_copy(gray[:, 0, :], gray[:, 2, :])
        v.tensor_copy(gray[:, WD + 1, :], gray[:, WD - 1, :]).then_inc(gray_set, 1)
        dve.wait_ge(gray_set, 1)
        link(v.tensor_tensor(gt[:, :, :], gray[:, 2:WD + 2, :], gray[:, 0:WD, :], ALU.subtract))
        absolute(gh[:, :, :], gt[:, :, :]).then_inc(gradh_set, 1)
        dve.wait_ge(gradh_set, 1)
        dve.wait_ge(diff_mm, 1)
        link(v.tensor_copy(gt[:, :, :].rearrange("h w b -> h (w b)"), bank[5][0:H, :]))
        link(absolute(gv[:, 1:WD + 1, :], gt[:, :, :]))
        link(v.tensor_copy(gv[:, 0, :], gv[:, 2, :]))
        link(v.tensor_copy(gv[:, WD + 1, :], gv[:, WD - 1, :]))
        half = WD // 2

        def weights(col, w0):
            return con[0:H, col + w0:col + w0 + half].unsqueeze(2).to_broadcast([H, half, B])

        for lo, w0 in ((0, 0), (half + 1, half)):
            dst = g4[:, 1, w0:w0 + half, :]
            link(v.tensor_tensor(gt[:, w0:w0 + half, :], gv[:, lo:lo + half, :], weights(C_WLO, w0), ALU.mult))
            link(v.tensor_tensor(dst, gv[:, lo + 1:lo + 1 + half, :], weights(C_WHI, w0), ALU.mult))
            link(v.tensor_tensor(dst, dst, gt[:, w0:w0 + half, :], ALU.add))
        dve.wait_ge(rows_mm, 1)
        link(v.tensor_copy(g4[:, 0].rearrange("h w b -> h (w b)"), bank[4][0:H, :]))
        link(v.tensor_tensor(g4[:, 2], g4[:, 0], g4[:, 1], ALU.add))
        link(v.tensor_scalar(g4[:, 2], g4[:, 2], 0.5, None, ALU.mult))
        link(v.tensor_tensor(g4[:, 3], g4[:, 0], g4[:, 1], ALU.subtract))
        link(absolute(g4[:, 3], g4[:, 3]))
        poolw = con[0:H, C_POOLW:C_POOLW + WD].unsqueeze(2).to_broadcast([H, WD, B])
        for k in range(4):
            ins = v.tensor_tensor(g4[:, k], g4[:, k], poolw, ALU.mult)
        link(ins)
        v.tensor_reduce(pooled[:, :, :], g4[:, :, :, :].rearrange("h k w b -> h k b w"), AX, ALU.add).then_inc(pooled_set, 1)
        dve.wait_ge(scores_mm, 1)
        v.tensor_copy(scores[:, :], bank[5][0:4, 0:B]).then_inc(scores_set, 1)
        dve.wait_ge(hid_mm, 1)
        v.tensor_scalar(hid1[:, :], bank[4][0:32, 0:B], mlpb1[:, 0:1], 0.0, ALU.add, ALU.max).then_inc(hid_set, 1)
        dve.wait_ge(logits_mm, 1)
        link(v.tensor_tensor(lg[:, 0:4], bank[5][0:B, 0:4], mlpb2[:, :], ALU.add))
        link(v.tensor_reduce(lg[:, 13:14], lg[:, 0:4], AX, ALU.max))
        v.tensor_scalar(lg[:, 12:13], lg[:, 13:14], -1.0, None, ALU.mult).then_inc(logits_set, 1)
        dve.wait_ge(exp_set, 1)
        link(v.tensor_reduce(lg[:, 14:15], lg[:, 4:8], AX, ALU.add))
        link(v.reciprocal(lg[:, 15:16], lg[:, 14:15]))
        link(v.tensor_scalar(lg[:, 8:12], lg[:, 4:8], lg[:, 15:16], None, ALU.mult))
        link(v.tensor_scalar(lg[:, 4:5], lg[:, 8:9], lg[:, 9:10], None, ALU.is_lt))
        link(v.tensor_scalar(lg[:, 5:7], lg[:, 10:12], lg[:, 9:10], None, ALU.is_le))
        link(v.tensor_tensor(lg[:, 7:8], lg[:, 5:6], lg[:, 6:7], ALU.mult))
        link(v.tensor_tensor(lg[:, 7:8], lg[:, 7:8], lg[:, 4:5], ALU.mult))
        v.tensor_scalar(diag[:, :], con[0:B, C_IDENT:C_IDENT + B], lg[:, 7:8], None, ALU.mult).then_inc(diag_set, 1)
        dve.wait_ge(mask_mm, 1)
        link(v.tensor_copy(mask[:, :], bank[4][:, 0:B]))
        dve.wait_ge(seq_set, 2 * B)
        dve.wait_ge(seqv_set, 2 * B)
        v.copy_predicated(seq[:, :, :], mask[:, :].unsqueeze(1).to_broadcast([P, L, B]), seq_v).then_inc(select_done, 1)

        dve.wait_ge(init_done, N_INIT)

        def add_output(j, d, ready, landed):
            dve.wait_ge(y_ready, ready)
            dve.wait_ge(tile_in[landed[0]], landed[1])
            kk = j if d == 0 else j * -1 + (NBLK - 1)
            t = tiles[:, bass.ds(kk, 1), :].rearrange("p a c -> p (a c)")
            v.tensor_tensor(t, Y[:, d * C:(d + 1) * C], t, ALU.add).then_inc(y_used, 1)

        def step(base, r):
            q, s, e, prev = r // TB, r % TB, r % 2, (r - 1) % RING
            turn = base + (r + 1)
            dve.wait_ge(reset_ready, turn)
            dve.wait_ge(hn_ready, turn)
            v.tensor_tensor_scan(cand[:, e * 2 * COLS:(e + 1) * 2 * COLS], rpair[:, e, :], NX[q][:, s * 2 * COLS:(s + 1) * 2 * COLS], 0.0,
                                 ALU.mult, ALU.add).then_inc(cand_pre, 1)
            dve.wait_ge(cand_ready, turn)
            dve.wait_ge(update_ready, turn)
            if not (isinstance(base, int) and base + r == 0):
                dve.wait_ge(neg_ready, base + r)
            v.tensor_tensor_scan(state[:, r, :], ztrip[:, e, :], state[:, prev, :], 0.0,
                                 ALU.mult, ALU.add).then_inc(state_ready, 1)
            new = state[:, r, :].rearrange("p (n k) -> p n k", k=3)
            hi = state[:, r, :].bitcast(BF16).rearrange("p (n k) -> p n k", k=6)[:, :, 5]
            dve.wait_ge(state_ready, turn)
            v.tensor_tensor(resid[:, e, :], new[:, :, 2], hi, ALU.subtract).then_inc(resid_ready, 1)
            dve.wait_ge(resid_ready, turn)
            v.tensor_tensor(low[:, e, :], resid[:, e, :],
                            resid[:, e, :].bitcast(BF16).rearrange("p (n k) -> p n k", k=2)[:, :, 1],
                            ALU.subtract).then_inc(low_ready, 1)
            v.tensor_scalar(new[:, :, 1], new[:, :, 2], -1.0, None, ALU.mult).then_inc(neg_ready, 1)

        def body(base, kblk, first, landed):
            for r in range(RING):
                q, s = r // TB, r % TB
                step(base, r)
                if s in (3, 5) and not first:
                    add_output(kblk + (q - 2), s // 4, kblk + (q - 1), landed[q])

        body(0, 0, True, None)
        with dve.Fori(1, NBLK // 4) as i:
            body(i * RING, i * 2, False, ((0, i * 32), (1, i * 32)))
        with dve.Fori(NBLK // 4, NBLK // 2) as i:
            body(i * RING, i * 2, False, ((0, 8 * NBLK), (1, 8 * NBLK)))
        for k in (NBLK - 2, NBLK - 1):
            for d in range(2):
                add_output(k, d, k + 1, (k % 2, 8 * NBLK))

    ctx.close()


def kernel(x, L0_conv_ln_gamma, L0_conv_ln_beta, L0_conv_mlp_w1, L0_conv_mlp_b1, L0_conv_mlp_w2, L0_conv_mlp_b2,
           L0_conv_in_w, L0_conv_in_b, L0_conv_gru_wih_f, L0_conv_gru_whh_f, L0_conv_gru_bih_f, L0_conv_gru_bhh_f,
           L0_conv_gru_wih_b, L0_conv_gru_whh_b, L0_conv_gru_bih_b, L0_conv_gru_bhh_b, L0_conv_out_w, L0_conv_out_b):
    import numpy as np
    import concourse.bacc as bacc
    from concourse.bass_utils import run_bass_kernel_spmd

    def both(f, b):
        return np.stack([np.asarray(f), np.asarray(b)])

    def turned(a):
        return np.ascontiguousarray(np.swapaxes(np.asarray(a), -1, -2))

    def column(a):
        return np.asarray(a)[:, None]

    arrays = {
        "x": x, "gamma": column(L0_conv_ln_gamma), "beta": column(L0_conv_ln_beta),
        "w1t": turned(L0_conv_mlp_w1), "b1": column(L0_conv_mlp_b1), "w2t": turned(L0_conv_mlp_w2), "b2": np.asarray(L0_conv_mlp_b2)[None, :],
        "in_w": L0_conv_in_w, "in_b": turned(np.asarray(L0_conv_in_b).reshape(DI // P, P)),
        "wiht": turned(both(L0_conv_gru_wih_f, L0_conv_gru_wih_b)),
        "whht": turned(both(L0_conv_gru_whh_f, L0_conv_gru_whh_b)),
        "bih": both(L0_conv_gru_bih_f, L0_conv_gru_bih_b)[:, None, :],
        "bhh": both(L0_conv_gru_bhh_f, L0_conv_gru_bhh_b)[:, None, :],
        "outwt": turned(L0_conv_out_w), "out_b": np.asarray(L0_conv_out_b)[None, :], "consts": shape_constants(),
    }
    nc = bacc.Bacc("TRN2", target_bir_lowering=False, num_devices=1)
    fed, aps = {}, []
    for name, a in arrays.items():
        a = np.ascontiguousarray(a)
        fed[f"in_{name}"] = a
        aps.append(nc.dram_tensor(f"in_{name}", a.shape, mybir.dt.from_np(a.dtype), kind="ExternalInput").ap())
    aps.append(nc.dram_tensor("out", (B, H, WD, C), F32, kind="ExternalOutput").ap())
    build(nc, *aps)
    got = run_bass_kernel_spmd(nc, [fed], core_ids=[0])
    return got.results[0]["out"]
```

```python
from contextlib import ExitStack

import concourse.bass as bass
from concourse import mybir

P = 128
B, H, WD, C = 16, 32, 32, 128
L = H * WD
DI = 2 * C
HID = 128
TB = 8
NBLK = L // TB
RING = 2 * TB
COLS = 2 * B
TPP = L // P
EDGE = 4 * TB
SLOTS = 4
JA = 2
HSCALE = 2.0 ** 14
EPS = 1e-5

F32 = mybir.dt.float32
BF16 = mybir.dt.bfloat16
F16 = mybir.dt.float16
I32 = mybir.dt.int32
ALU = mybir.AluOpType
ACT = mybir.ActivationFunctionType
AX = mybir.AxisListType.X
G_R, G_Z, G_N, G_HN = range(4)

C_IDENT = 0
C_SELECT = C_IDENT + P
C_MEAN = C_SELECT + P
C_DIFF = C_MEAN + H
C_RESIZE = C_DIFF + H
C_POOLH = C_RESIZE + H
C_WLO = C_POOLH + 16
C_WHI = C_WLO + WD
C_POOLW = C_WHI + WD
C_ONES = C_POOLW + WD
C_IND = C_ONES + P
C_END = C_IND + 2 * P


def shape_constants():
    import numpy as np

    t = np.zeros((P, C_END), np.float32)
    t[:, C_IDENT:C_IDENT + P] = np.eye(P)
    ppr = P // H
    for p in range(P):
        t[p, C_SELECT + (p % ppr) * H + p // ppr] = 1.0 / C
    t[:, C_MEAN:C_MEAN + H] = 1.0 / C
    for i in range(1, H - 1):
        t[i + 1, C_DIFF + i] += 1.0
        t[i - 1, C_DIFF + i] -= 1.0
    for i in range(H):
        src = min(max((i + 0.5) * (H + 2) / H - 0.5, 0.0), H + 1)
        lo = int(np.floor(src))
        w = src - lo
        for k, v in ((lo, 1.0 - w), (min(lo + 1, H + 1), w)):
            row = k - 1
            row = -row if row < 0 else (2 * (H - 1) - row if row > H - 1 else row)
            t[row, C_RESIZE + i] += v
        t[:, C_WLO + i] = 1.0 - w
        t[:, C_WHI + i] = w
        edge = 2.0 if i in (0, H - 1) else 3.0
        for k in range(4):
            t[i, C_POOLH + 4 * k + k] = edge / (9.0 * H * WD)
        t[:, C_POOLW + i] = edge
    t[:, C_ONES:C_ONES + P] = 1.0
    ind = t[:, C_IND:C_IND + 2 * P].reshape(P, TB, 2, B)
    for part in range(3):
        for d in range(2):
            ind[3 * d + part, :, d, :] = 1.0
    t[:, C_IND:C_IND + 2 * P] = ind.reshape(P, 2 * P)
    return t


def build(nc, x, gamma, beta, w1t, b1, w2t, b2, in_w, in_b, wiht, whht, bih, bhh, outwt, out_b, consts, out):
    ctx = ExitStack()

    def sb(name, shape, dt=F32):
        return ctx.enter_context(nc.sbuf_tensor(name, shape, dt))

    def sem(name):
        return ctx.enter_context(nc.semaphore(name))

    seq = sb("seq", [P, L, B])
    big = sb("big", [P, L * B])
    seq_v = big[:, :].rearrange("c (t b) -> c t b", b=B)
    tiles = big[:, :].rearrange("p (k c) -> p k c", c=C)
    xin = sb("xin", [P, SLOTS, TPP, C])
    stats = sb("stats", [P, SLOTS, TPP, 6])
    moments = sb("moments", [P, SLOTS, TPP, 2])
    std = sb("std", [P, SLOTS, TPP])
    rstd = sb("rstd", [P, SLOTS, TPP])
    shift = sb("shift", [P, SLOTS, TPP])
    gamma_row = sb("gamma_row", [P, C])
    weighted = sb("weighted", [P, TPP, C])
    gray_tok = sb("gray_tok", [P, B, TPP])
    beta_mean = sb("beta_mean", [H, 1])
    gb = sb("gb", [P, 2])
    eps = sb("eps", [P, 1])
    table = sb("table", [P, 1])
    con = sb("con", [P, C_END])
    ind = sb("ind", [6, 2 * P], BF16)
    inw = sb("inw", [P, DI // P, C])
    inb = sb("inb", [P, DI // P])
    wih = sb("wih", [P, 2, DI // P, 3 * HID])
    whh = sb("whh", [P, 2, 3 * HID])
    wsplit = sb("wsplit", [P, 3, 2, 3 * HID], BF16)
    wcomb = sb("wcomb", [P, 2, 3 * HID])
    outw = sb("outw", [P, 2, C])
    bfold = sb("bfold", [P, 2, 3])
    bih_col = sb("bih_col", [P, 2, 3])
    bhh_col = sb("bhh_col", [P, 2, 3])
    bias_col = sb("bias_col", [P, 9])
    bias_bf = sb("bias_bf", [P, 3, 9], BF16)
    bias_part = sb("bias_part", [P, 9 * 3])
    bias6 = sb("bias6", [6, 4 * HID], BF16)
    obias = sb("obias", [3, C], BF16)
    ones3 = sb("ones3", [3, P], BF16)
    mlp1 = sb("mlp1", [4, 32])
    mlpb1 = sb("mlpb1", [32, 1])
    mlp2 = sb("mlp2", [32, 4])
    mlpb2 = sb("mlpb2", [B, 4])
    g4 = xin[0:H, 0:2].rearrange("h q j c -> h (q j c)").rearrange("h (k w b) -> h k w b", k=4, b=B)
    spare = xin[0:H, 2:4].rearrange("h q j c -> h (q j c)").rearrange("h (w b) -> h w b", b=B)
    gray, gv, gh = spare[:, 0:WD + 2], spare[:, WD + 2:2 * WD + 4], spare[:, 2 * WD + 4:3 * WD + 4]
    gt = sb("gt", [H, WD, B])
    pooled = sb("pooled", [H, 4, B])
    scores = sb("scores", [4, B])
    hid1 = sb("hid1", [32, B])
    lg = sb("lg", [B, 16])
    diag = sb("diag", [B, B])
    mask = sb("mask", [P, B], I32)
    rev = sb("rev", [P, 2, TB, B])
    hist = sb("hist", [P, 2, 2, B, TB])
    state = sb("state", [P, RING, 3 * COLS])
    resid = sb("resid", [P, 2, COLS])
    low = sb("low", [P, 2, COLS], BF16)
    half_hi = sb("half_hi", [P, 2, COLS], F16)
    half_lo = sb("half_lo", [P, 2, COLS], F16)
    rpair = sb("rpair", [P, 2, 2 * COLS])
    ztrip = sb("ztrip", [P, 2, 3 * COLS])

    bank = [ctx.enter_context(nc.psum_tensor(f"bank{i}", [P, 512], F32)) for i in range(8)]
    R, Z, NX, Y = bank[0:2], bank[2:4], bank[4:6], bank[6]
    cand = bank[7]

    w_in = sem("w_in")
    first_in = sem("first_in")
    x_in = [sem(f"x_in{q}") for q in range(SLOTS)]
    stats_set = sem("stats_set")
    moments_set = sem("moments_set")
    std_set = sem("std_set")
    rstd_set = sem("rstd_set")
    shift_set = sem("shift_set")
    xhat_act = sem("xhat_act")
    xhat_pool = sem("xhat_pool")
    gray_sum = sem("gray_sum")
    beta_mm = sem("beta_mm")
    select_rest = sem("select_rest")
    fold_set = sem("fold_set")
    link_g = sem("link_g")
    xT_set = sem("xT_set")
    seq_set = sem("seq_set")
    w_mm = sem("w_mm")
    link_v = sem("link_v")
    bias_split = sem("bias_split")
    bias_mm = sem("bias_mm")
    bias_rows = sem("bias_rows")
    cast_set = sem("cast_set")
    weights_set = sem("weights_set")
    gray_mm = sem("gray_mm")
    gray_set = sem("gray_set")
    diff_mm = sem("diff_mm")
    gradh_set = sem("gradh_set")
    rows_mm = sem("rows_mm")
    gradv_set = sem("gradv_set")
    cols_set = sem("cols_set")
    pooled_set = sem("pooled_set")
    scores_mm = sem("scores_mm")
    scores_set = sem("scores_set")
    hid_mm = sem("hid_mm")
    hid_set = sem("hid_set")
    logits_mm = sem("logits_mm")
    logits_set = sem("logits_set")
    exp_set = sem("exp_set")
    diag_set = sem("diag_set")
    mask_mm = sem("mask_mm")
    select_done = sem("select_done")
    init_done = sem("init_done")
    reset_pre = sem("reset_pre")
    hn_ready = sem("hn_ready")
    update_pre = sem("update_pre")
    reset_ready = sem("reset_ready")
    update_ready = sem("update_ready")
    cand_pre = sem("cand_pre")
    cand_ready = sem("cand_ready")
    state_ready = sem("state_ready")
    resid_ready = sem("resid_ready")
    low_ready = sem("low_ready")
    half_hi_ready = sem("half_hi_ready")
    half_lo_ready = sem("half_lo_ready")
    neg_ready = sem("neg_ready")
    hist_ready = sem("hist_ready")
    rev_ready = sem("rev_ready")
    images_counted = sem("images_counted")
    tokens_counted = sem("tokens_counted")
    blocks_counted = sem("blocks_counted")
    y_ready = sem("y_ready")
    y_used = sem("y_used")
    tile_in0 = sem("tile_in0")
    tile_in1 = sem("tile_in1")
    out_done = sem("out_done")
    tile_in = (tile_in0, tile_in1)

    x_tok = x.rearrange("b h w c -> b (h w) c")
    out_tok = out.rearrange("b h w c -> b (h w) c")
    x_part = x_tok.rearrange("b (p j) c -> b p (j c)", j=TPP)

    N_PARAM = 15
    N_FIRST = 4

    def ahead(rnd, q, o):
        return rnd + (q + o) // SLOTS, (q + o) % SLOTS, rnd * SLOTS + (q + o + 1)

    block = ctx.enter_context(nc.Block())

    @block.sync
    def _(sp):
        def load_image(rnd, q, wait):
            b = rnd * SLOTS + q
            if wait:
                sp.wait_ge(gray_sum, b + (1 - SLOTS))
                sp.wait_ge(xT_set, b * 2 + (2 - 2 * SLOTS))
            sp.dma_start(xin[:, q].rearrange("p j c -> p (j c)"),
                         x_part[bass.ds(b, 1)].rearrange("a p n -> (a p) n") if not isinstance(b, int) else x_part[b]
                         ).then_inc(x_in[q], 16)

        load_image(0, 0, False)
        load_image(0, 1, False)
        for dst, src in ((con[:, :], consts), (gb[:, 0:1], gamma), (gb[:, 1:2], beta),
                         (gamma_row[:, :], gamma.rearrange("c a -> a c").to_broadcast((P, C)))):
            sp.dma_start(dst, src).then_inc(first_in, 16)
        load_image(0, 2, False)
        load_image(0, 3, False)
        params = (
            (inw[:, :, :], in_w.rearrange("(k p) c -> p k c", p=P)),
            (inb[:, :], in_b),
            (wih[:, 0], wiht[0].rearrange("(k p) m -> p k m", p=P)),
            (wih[:, 1], wiht[1].rearrange("(k p) m -> p k m", p=P)),
            (whh[:, 0], whht[0]), (whh[:, 1], whht[1]),
            (outw[:, 0], outwt[0:HID]), (outw[:, 1], outwt[HID:2 * HID]),
            (mlp1[:, :], w1t), (mlpb1[:, :], b1), (mlp2[:, :], w2t),
            (mlpb2[:, :], b2.to_broadcast((B, 4))),
            (bih_col[:, :, :], bih), (bhh_col[:, :, :], bhh), (bias_col[:, 8:9], out_b),
        )
        assert len(params) == N_PARAM
        for q in range(SLOTS):
            load_image(1, q, True)
            for dst, src in params[q * 4:q * 4 + 4]:
                sp.dma_start(dst, src).then_inc(w_in, 16)
        with sp.Fori(2, B // SLOTS) as i:
            for q in range(SLOTS):
                load_image(i, q, True)
        sp.wait_ge(select_done, 1)

        def tile_rows(t, k):
            return t[:, bass.ds(k * TB, TB), :]

        def load_tiles(k, q, wait):
            if wait is not None:
                sp.wait_ge(y_used, wait)
            for kk in (k, k * -1 + (NBLK - 1)):
                sp.dma_start(tiles[:, bass.ds(kk, 1), :].rearrange("p a c -> p (a c)"),
                             tile_rows(x_tok, kk)).then_inc(tile_in[q], 16)

        load_tiles(0, 0, None)
        load_tiles(1, 1, None)
        sp.wait_ge(select_rest, 1)
        with sp.Fori(1, NBLK // 4) as i:
            for q in range(2):
                load_tiles(i * 2 + q, q, i * 4 + (2 * q - 2))
        with sp.Fori(NBLK // 4, NBLK // 2) as i:
            for q in range(2):
                for d in range(2):
                    k = i * 2 + q
                    kk = k if d == 0 else k * -1 + (NBLK - 1)
                    sp.wait_ge(y_used, i * 4 + (2 * q + d + 1))
                    sp.dma_start(tile_rows(out_tok, kk),
                                 tiles[:, bass.ds(kk, 1), :].rearrange("p a c -> p (a c)")).then_inc(out_done, 16)
        sp.wait_ge(out_done, 16 * NBLK)

    N_INIT = 9

    @block.gpsimd
    def _(g):
        g.memset(rpair[:, :, :], 0.0).then_inc(init_done, 1)
        g.memset(ztrip[:, :, :], 0.0).then_inc(init_done, 1)
        g.memset(state[:, :, :], 0.0).then_inc(init_done, 1)
        g.memset(resid[:, :, :], 0.0).then_inc(init_done, 1)
        g.memset(low[:, :, :], 0.0).then_inc(init_done, 1)
        g.memset(half_hi[:, :, :], 0.0).then_inc(init_done, 1)
        g.memset(half_lo[:, :, :], 0.0).then_inc(init_done, 1)
        g.wait_ge(init_done, 7)
        for q in range(2):
            g.memset(ztrip[:, q, :].rearrange("p (n e) -> p n e", e=3)[:, :, 1], 1.0).then_inc(init_done, 1)
        def normalise(rnd, q):
            turn = ahead(rnd, q, 0)[2]
            g.wait_ge(shift_set, turn)
            g.sem_inc(tokens_counted, 1)
            for j in range(JA, TPP):
                ins = g.tensor_scalar(xin[:, q, j, :], xin[:, q, j, :], rstd[:, q, j:j + 1], shift[:, q, j:j + 1],
                                      ALU.mult, ALU.add)
            ins.then_inc(xhat_pool, 1)

        g.wait_ge(first_in, 16 * N_FIRST)
        for q in range(SLOTS):
            normalise(0, q)
        with g.Fori(1, B // SLOTS) as i:
            for q in range(SLOTS):
                normalise(i, q)

        links = [0]

        def link(ins):
            links[0] += 1
            ins.then_inc(link_g, 1)
            g.wait_ge(link_g, links[0])

        g.wait_ge(w_in, 16 * N_PARAM)
        g.wait_ge(fold_set, 1)
        total = bias_col[:, 0:8].rearrange("p (g d) -> p d g", d=2)
        link(g.tensor_tensor(total[:, :, 0:3], bfold[:, :, :], bih_col[:, :, :], ALU.add))
        link(g.tensor_tensor(total[:, :, 0:2], total[:, :, 0:2], bhh_col[:, :, 0:2], ALU.add))
        link(g.tensor_copy(total[:, :, 3], bhh_col[:, :, 2]))
        for k in range(3):
            link(g.tensor_copy(bias_bf[:, k, :], bias_col[:, :]))
            if k < 2:
                link(g.tensor_tensor(bias_col[:, :], bias_col[:, :], bias_bf[:, k, :], ALU.subtract))
        g.tensor_copy(bias_part[:, :].rearrange("p (n k) -> p k n", k=3), bias_bf[:, :, :]).then_inc(bias_split, 1)
        g.tensor_copy(ind[:, :], con[0:6, C_IND:C_IND + 2 * P]).then_inc(cast_set, 1)
        scaled = whh[:, :, G_Z * HID:(G_N + 1) * HID]
        link(g.tensor_scalar(scaled, scaled, 1.0 / HSCALE, None, ALU.mult))
        w_all = whh[:, :, :].rearrange("p d n -> p (d n)")
        parts = [wsplit[:, k].rearrange("p d n -> p (d n)") for k in range(3)]
        link(g.tensor_copy(parts[0], w_all))
        link(g.tensor_tensor(w_all, w_all, parts[0], ALU.subtract))
        link(g.tensor_copy(parts[1], w_all))
        link(g.tensor_tensor(w_all, w_all, parts[1], ALU.subtract))
        g.tensor_copy(parts[2], w_all).then_inc(weights_set, 1)

        def reorder(k, q, wait):
            g.wait_ge(state_ready, (k + 1) * TB)
            if wait:
                g.wait_ge(y_ready, k - 1)
            g.sem_inc(blocks_counted, 1)
            for d in range(2):
                h = state[:, q * TB:(q + 1) * TB, :].rearrange("p s (d b k) -> p s d b k", d=2, k=3)[:, :, d, :, 2]
                if d == 0:
                    ins = g.tensor_copy(hist[:, q, d], h.rearrange("p s b -> p b s"))
                else:
                    for s in range(TB):
                        ins = g.tensor_copy(hist[:, q, d, :, TB - 1 - s], h[:, s, :])
            ins.then_inc(hist_ready, 1)

        def reverse(k, q):
            for s in range(TB):
                ins = g.tensor_copy(rev[:, q, s, :], seq[:, bass.ds(k * -TB + (L - 1 - s), 1), :].rearrange("c a b -> c (a b)"))
            ins.then_inc(rev_ready, 1)

        g.wait_ge(select_done, 1)
        for q in range(2):
            reverse(q, q)
        for q in range(2):
            reorder(q, q, False)
            reverse(q + 2, q)
        g.wait_ge(select_rest, 1)
        with g.Fori(1, NBLK // 2 - 1) as i:
            for q in range(2):
                reorder(i * 2 + q, q, True)
                reverse(i * 2 + (q + 2), q)
        for q in range(2):
            reorder(NBLK - 2 + q, q, True)

    @block.scalar
    def _(act):
        def deviation(rnd, q, o):
            _, qo, turn = ahead(rnd, q, o)
            act.wait_ge(moments_set, turn)
            act.activation(std[:, qo, :], moments[:, qo, :, 1], ACT.Sqrt, bias=eps[:, 0:1]).then_inc(std_set, 1)

        def normalise(rnd, q):
            act.wait_ge(shift_set, ahead(rnd, q, 0)[2])
            for j in range(JA):
                ins = act.activation(xin[:, q, j, :], xin[:, q, j, :], ACT.Identity,
                                     bias=shift[:, q, j:j + 1], scale=rstd[:, q, j:j + 1])
            ins.then_inc(xhat_act, 1)

        def evacuate(rnd, q, halves=(0, 1)):
            _, q1, turn = ahead(rnd, q, -1)
            for half in halves:
                act.wait_ge(xT_set, turn * 2 + (half - 1))
                src = bank[2 * (q1 % 2) + half]
                dst = seq[:, :, :].rearrange("c (p j) b -> c j p b", j=TPP)[:, 4 * half:4 * half + 4, :, bass.ds(turn - 1, 1)]
                act.activation(dst.rearrange("c j p b -> c j (p b)"), src[:, :].rearrange("c (j p) -> c j p", j=4),
                               ACT.Identity, bias=gb[:, 1:2], scale=gb[:, 0:1])
                dst = seq_v.rearrange("c (m j h) b -> c j h m b", m=WD // TPP, j=TPP)[
                    :, 4 * half:4 * half + 4, :, :, bass.ds(turn - 1, 1)].rearrange("c j h m b -> c j h (m b)")
                act.activation(dst, src[:, :].rearrange("c (j h m) -> c j h m", j=4, m=WD // TPP),
                               ACT.Identity, bias=gb[:, 1:2], scale=gb[:, 0:1]).then_inc(seq_set, 1)

        def image(rnd, q, first=False, last=False):
            normalise(rnd, q)
            if not (first and q == 0):
                evacuate(rnd, q, (0,))
            if not (last and q == SLOTS - 1):
                deviation(rnd, q, 1)
            if not (first and q == 0):
                evacuate(rnd, q, (1,))

        act.wait_ge(cast_set, 1)
        deviation(0, 0, 0)
        act.wait_ge(first_in, 16 * N_FIRST)
        for q in range(SLOTS):
            image(0, q, first=True)
        with act.Fori(1, B // SLOTS - 1) as i:
            for q in range(SLOTS):
                image(i, q)
        for q in range(SLOTS):
            image(B // SLOTS - 1, q, last=True)
        evacuate(B // SLOTS, 0)
        act.wait_ge(w_mm, 1)
        for d in range(2):
            ins = act.copy(bfold[:, d, :], bank[6 + d][:, 3 * HID:3 * HID + 3])
        ins.then_inc(fold_set, 1)
        for d in range(2):
            act.copy(wcomb[:, d, :], bank[6 + d][:, 0:3 * HID]).then_inc(fold_set, 1)
        act.wait_ge(bias_mm, 1)
        act.copy(bias6[:, :], bank[0][0:6, :])
        act.copy(obias[:, :], bank[1][0:3, 0:C]).then_inc(bias_rows, 1)

        act.wait_ge(logits_set, 1)
        act.activation(lg[:, 4:8], lg[:, 0:4], ACT.Exp, bias=lg[:, 12:13]).then_inc(exp_set, 1)
        act.activation(table[:, :], eps[:, :], ACT.Sigmoid)

        act.wait_ge(init_done, N_INIT)

        def body(base):
            for r in range(RING):
                q, s, e = r // TB, r % TB, r % 2
                turn = base + (r + 1)
                act.wait_ge(reset_pre, turn)
                act.activation(rpair[:, e, :].rearrange("p (d n k) -> p d n k", d=2, k=2)[:, :, :, 1],
                               R[q][:, s * COLS:(s + 1) * COLS].rearrange("p (d b) -> p d b", d=2), ACT.Sigmoid).then_inc(reset_ready, 1)
                act.wait_ge(update_pre, turn)
                act.activation(ztrip[:, e, :].rearrange("p (d n k) -> p d n k", d=2, k=3)[:, :, :, 2],
                               Z[q][:, s * COLS:(s + 1) * COLS].rearrange("p (d b) -> p d b", d=2), ACT.Sigmoid, scale=-1.0).then_inc(update_ready, 1)
                act.wait_ge(cand_pre, turn)
                act.activation(state[:, (r - 1) % RING, :].rearrange("p (n k) -> p n k", k=3)[:, :, 0],
                               cand[:, e * 2 * COLS:(e + 1) * 2 * COLS].rearrange("p (n k) -> p n k", k=2)[:, :, 1],
                               ACT.Tanh).then_inc(cand_ready, 1)

        body(0)
        with act.Fori(1, L // RING) as i:
            body(i * RING)

    @block.tensor
    def _(pe):
        identity = con[:, C_IDENT:C_IDENT + P]

        def transposes(rnd, q, first=False):
            turn = ahead(rnd, q, 0)[2]
            for half in range(2):
                if half == 0:
                    pe.wait_ge(xhat_pool, turn)
                    pe.wait_ge(xhat_act, turn)
                if not (first and q < 2):
                    pe.wait_ge(seq_set, turn * 2 + (half - 5))
                for j in range(4):
                    ins = nc.tensor.transpose(bank[2 * (q % 2) + half][:, j * P:(j + 1) * P],
                                              xin[:, q, 4 * half + j, :], identity)
                ins.then_inc(xT_set, 1)

        pe.wait_ge(first_in, 16 * N_FIRST)
        for q in range(SLOTS):
            transposes(0, q, True)
        for q in range(SLOTS):
            transposes(1, q)
        pe.wait_ge(w_in, 16 * N_PARAM)
        for d in range(2):
            for k in range(DI // P):
                nc.tensor.matmul(bank[6 + d][:, 0:3 * HID], inw[:, k, :], wih[:, d, k, :],
                                 start=(k == 0), stop=(k == DI // P - 1))
            for g in range(3):
                for k in range(DI // P):
                    ins = nc.tensor.matmul(bank[6 + d][:, 3 * HID + g:3 * HID + g + 1],
                                           wih[:, d, k, g * HID:(g + 1) * HID], inb[:, k:k + 1],
                                           start=False, stop=(k == DI // P - 1), skip_group_check=True)
        ins.then_inc(w_mm, 1)
        with pe.Fori(2, B // SLOTS) as i:
            for q in range(SLOTS):
                transposes(i, q)

        pe.wait_ge(gray_sum, B)
        for k in range(P // H):
            nc.tensor.matmul(bank[4][0:H, k * P:(k + 1) * P], con[:, C_SELECT + k * H:C_SELECT + (k + 1) * H],
                             gray_tok[:, :, :].rearrange("p b j -> p (b j)"), start=True, stop=True)
        nc.tensor.matmul(bank[5][0:H, 0:1], con[:, C_MEAN:C_MEAN + H], gb[:, 1:2], start=True, stop=True).then_inc(gray_mm, 1)
        pe.wait_ge(gray_set, 1)
        nc.tensor.matmul(bank[5][0:H, :], con[0:H, C_DIFF:C_DIFF + H],
                         gray[:, 1:WD + 1, :].rearrange("h w b -> h (w b)"), start=True, stop=True).then_inc(diff_mm, 1)
        pe.wait_ge(gradh_set, 1)
        nc.tensor.matmul(bank[4][0:H, :], con[0:H, C_RESIZE:C_RESIZE + H],
                         gh[:, :, :].rearrange("h w b -> h (w b)"), start=True, stop=True).then_inc(rows_mm, 1)
        pe.wait_ge(bias_split, 1)
        pe.wait_ge(seq_set, 2 * B)
        for g in range(4):
            nc.tensor.transpose(bank[0][0:6, g * HID:(g + 1) * HID], bias_part[:, 6 * g:6 * g + 6], identity)
        nc.tensor.transpose(bank[1][0:3, 0:C], bias_part[:, 24:27], identity).then_inc(bias_mm, 1)
        pe.wait_ge(pooled_set, 1)
        for k, at in enumerate((0, 1, 3, 2)):
            ins = nc.tensor.matmul(bank[5][0:4, 0:B], con[0:H, C_POOLH + 4 * k:C_POOLH + 4 * k + 4],
                                   pooled[:, at, :], start=(k == 0), stop=(k == 3))
        ins.then_inc(scores_mm, 1)
        pe.wait_ge(scores_set, 1)
        nc.tensor.matmul(bank[4][0:32, 0:B], mlp1[:, :], scores[:, :], start=True, stop=True).then_inc(hid_mm, 1)
        pe.wait_ge(hid_set, 1)
        nc.tensor.matmul(bank[5][0:B, 0:4], hid1[:, :], mlp2[:, :], start=True, stop=True).then_inc(logits_mm, 1)
        pe.wait_ge(diag_set, 1)
        pe.wait_ge(fold_set, 3)
        nc.tensor.matmul(bank[7][:, 0:B], con[0:B, C_ONES:C_ONES + P], diag[:, :], start=True, stop=True).then_inc(mask_mm, 1)

        def mm(o, w, m, start=False):
            return nc.tensor.matmul(o, w, m, start=start, stop=True, skip_group_check=True)

        def nx(q):
            return NX[q][:, :].rearrange("p (s d b k) -> p s d b k", s=TB, d=2, k=2)

        def gate(banks, q):
            return banks[q][:, 0:TB * COLS].rearrange("p (s d b) -> p s d b", s=TB, d=2)

        def fill_bias(q, which):
            if which in (G_R, G_Z):
                bk = (R if which == G_R else Z)[q]
                return mm(bk[:, 0:2 * TB * B], bias6[:, which * HID:(which + 1) * HID],
                          ind[:, :], start=True)
            k = 0 if which == G_HN else 1
            return mm(NX[q][:, k::2], bias6[:, which * HID:(which + 1) * HID],
                      ind[:, :], start=(which == G_HN))

        def fill_input(q, kblk, g, d):
            src = seq[:, bass.ds(kblk * TB, TB), :] if d == 0 else rev[:, q]
            w = wcomb[:, d, g * HID:(g + 1) * HID]
            if g == G_N:
                return mm(nx(q)[:, :, d, :, 1], w, src)
            return mm(gate(R if g == G_R else Z, q)[:, :, d, :], w, src)

        FILL = [[("b", G_R)], [("b", G_Z), (G_R, 0)], [("b", G_HN), (G_Z, 0)], [("b", G_N), (G_N, 0)],
                [(G_R, 1)], [(G_Z, 1)], [(G_N, 1)], []]
        FIRST_BACKWARD = 4

        def fill(q, kblk, items, rev_turn=None):
            if rev_turn is not None:
                pe.wait_ge(rev_ready, rev_turn)
            for it in items:
                if it[0] == "b":
                    fill_bias(q, it[1])
                else:
                    fill_input(q, kblk, *it)

        def project(q, d):
            return mm(Y[:, d * C:(d + 1) * C], hist[:, q, d].rearrange("p b s -> p (b s)"), outw[:, d, :],
                      start=(d == 0))

        def project_forward(q):
            project(q, 0)
            return mm(Y[:, 0:C], ones3[:, :], obias[:, :])

        def step(base, r):
            q, s, e = r // TB, r % TB, r % 2
            prev = (r - 1) % RING
            h0 = state[:, prev, :].bitcast(BF16).rearrange("p (d b k) -> p d b k", d=2, k=6)[:, :, :, 5]
            h1 = resid[:, 1 - e, :].bitcast(BF16).rearrange("p (d b k) -> p d b k", d=2, k=2)[:, :, :, 1]
            h2 = low[:, 1 - e, :].rearrange("p (d b) -> p d b", d=2)
            hi = half_hi[:, 1 - e, :].rearrange("p (d b) -> p d b", d=2)
            lo = half_lo[:, 1 - e, :].rearrange("p (d b) -> p d b", d=2)

            def dst(g, d):
                if g == G_N:
                    return nx(q)[:, s, d, :, 0]
                return gate(R if g == G_R else Z, q)[:, s, d, :]

            def run(g, d, k, hp):
                return mm(dst(g, d), wsplit[:, k, d, g * HID:(g + 1) * HID], hp[:, d, :])

            step0 = isinstance(base, int) and base + r == 0
            if not step0:
                pe.wait_ge(state_ready, base + r)
            for d in range(2):
                for k in range(3):
                    run(G_R, d, k, h0)
            if not step0:
                pe.wait_ge(resid_ready, base + r)
            for d in range(2):
                for k in range(2):
                    run(G_R, d, k, h1)
            if not step0:
                pe.wait_ge(half_hi_ready, base + r)
            for d in range(2):
                for k in range(2):
                    run(G_N, d, k, hi)
            if not step0:
                pe.wait_ge(low_ready, base + r)
            for d in range(2):
                ins = run(G_R, d, 0, h2)
            ins.then_inc(reset_pre, 1)
            for d in range(2):
                run(G_N, d, 2, hi)
            if not step0:
                pe.wait_ge(half_lo_ready, base + r)
            for d in range(2):
                for k in range(2):
                    ins = run(G_N, d, k, lo)
            ins.then_inc(hn_ready, 1)
            for d in range(2):
                for k in range(3):
                    run(G_Z, d, k, hi)
                for k in range(2):
                    ins = run(G_Z, d, k, lo)
            ins.then_inc(update_pre, 1)

        def body(base, kblk, first=False, last=False):
            for r in range(RING):
                q, s = r // TB, r % TB
                step(base, r)
                if not (last and q == 1):
                    fill(1 - q, kblk + (q + 1), FILL[s], kblk + (q + 2) if s == FIRST_BACKWARD else None)
                if s == TB - 1 and not (first and q == 0):
                    if not (first and q == 1):
                        pe.wait_ge(y_used, (kblk + (q - 1)) * 2)
                    pe.wait_ge(hist_ready, kblk + q)
                    project_forward(1 - q)
                if s == 0 and not (first and q == 0) and not (first and q == 1):
                    project(q, 1).then_inc(y_ready, 1)

        pe.wait_ge(bias_rows, 1)
        pe.wait_ge(cast_set, 2)
        pe.wait_ge(weights_set, 1)
        pe.wait_ge(init_done, N_INIT)
        for g in (G_R, G_Z, G_HN, G_N):
            fill_bias(0, g)
        pe.wait_ge(select_done, 1)
        for g in (G_R, G_N, G_Z):
            fill_input(0, 0, g, 0)
        pe.wait_ge(rev_ready, 1)
        for g in (G_R, G_N, G_Z):
            fill_input(0, 0, g, 1)
        body(0, 0, first=True)
        pe.wait_ge(select_rest, 1)
        with pe.Fori(1, L // RING - 1) as i:
            body(i * RING, i * 2)
        body(L - RING, NBLK - 2, last=True)
        project(0, 1).then_inc(y_ready, 1)
        pe.wait_ge(y_used, 2 * (NBLK - 1))
        pe.wait_ge(hist_ready, NBLK)
        project_forward(1)
        project(1, 1).then_inc(y_ready, 1)

    @block.vector
    def _(dve):
        v = nc.vector
        links = [0]

        def link(ins):
            links[0] += 1
            ins.then_inc(link_v, 1)
            dve.wait_ge(link_v, links[0])

        link(v.memset(ones3[:, :], 1.0))
        v.memset(eps[:, :], EPS).then_inc(cast_set, 1)

        def statistics(rnd, q, o):
            r1, q1, turn = ahead(rnd, q, o)
            dve.wait_ge(x_in[q1], r1 * 16 + 16)
            for j in range(TPP):
                ins = v.bn_stats(out=stats[:, q1, j, :], in_=xin[:, q1, j, :])
            ins.then_inc(stats_set, 1)
            dve.wait_ge(stats_set, turn)
            dve.sem_inc(images_counted, 1)
            for j in range(TPP):
                ins = v.bn_aggr(out=moments[:, q1, j, :], in_=stats[:, q1, j, :])
            ins.then_inc(moments_set, 1)

        def scales(rnd, q, o):
            _, q1, turn = ahead(rnd, q, o)
            dve.wait_ge(std_set, turn)
            v.reciprocal(rstd[:, q1, :], std[:, q1, :]).then_inc(rstd_set, 1)
            dve.wait_ge(rstd_set, turn)
            dve.wait_ge(moments_set, turn)
            v.scalar_tensor_tensor(out=shift[:, q1, :], in0=moments[:, q1, :, 0], scalar=-1.0, in1=rstd[:, q1, :],
                                   op0=ALU.mult, op1=ALU.mult).then_inc(shift_set, 1)

        def gray_sums(rnd, q):
            _, q1, turn = ahead(rnd, q, -1)
            dve.wait_ge(xhat_act, turn)
            dve.wait_ge(xhat_pool, turn)
            if not (isinstance(rnd, int) and turn == 1):
                dve.wait_ge(gray_sum, turn - 1)
            for j in range(TPP):
                ins = v.scalar_tensor_tensor(out=weighted[:, j, :], in0=xin[:, q1, j, :], scalar=1.0, in1=gamma_row[:, :],
                                             op0=ALU.mult, op1=ALU.mult,
                                             accum_out=gray_tok[:, bass.ds(turn - 1, 1), j:j + 1].rearrange("p a b -> p (a b)"))
            ins.then_inc(gray_sum, 1)

        def image(rnd, q, first=False, last=False):
            if not (last and q == SLOTS - 1):
                statistics(rnd, q, 1)
            if not (first and q == 0):
                gray_sums(rnd, q)
            if not (last and q == SLOTS - 1):
                scales(rnd, q, 1)

        statistics(0, 0, 0)
        scales(0, 0, 0)
        dve.wait_ge(first_in, 16 * N_FIRST)
        for q in range(SLOTS):
            image(0, q, first=True)
        with dve.Fori(1, B // SLOTS - 1) as i:
            for q in range(SLOTS):
                image(i, q)
        for q in range(SLOTS):
            image(B // SLOTS - 1, q, last=True)
        gray_sums(B // SLOTS, 0)

        def absolute(dst, src):
            return v.scalar_tensor_tensor(out=dst, in0=src, scalar=-1.0, in1=src, op0=ALU.mult, op1=ALU.max)

        dve.wait_ge(gray_mm, 1)
        link(v.tensor_copy(beta_mean[:, :], bank[5][0:H, 0:1]))
        link(v.tensor_scalar(gray[:, 1:WD + 1, :].rearrange("h (k j) b -> h k b j", j=TPP),
                             bank[4][0:H, :].rearrange("h (k b j) -> h k b j", b=B, j=TPP),
                             beta_mean[:, 0:1], None, ALU.add))
        v.tensor_copy(gray[:, 0, :], gray[:, 2, :])
        v.tensor_copy(gray[:, WD + 1, :], gray[:, WD - 1, :]).then_inc(gray_set, 1)
        dve.wait_ge(gray_set, 1)
        link(v.tensor_tensor(gt[:, :, :], gray[:, 2:WD + 2, :], gray[:, 0:WD, :], ALU.subtract))
        absolute(gh[:, :, :], gt[:, :, :]).then_inc(gradh_set, 1)
        dve.wait_ge(gradh_set, 1)
        dve.wait_ge(diff_mm, 1)
        link(v.tensor_copy(gt[:, :, :].rearrange("h w b -> h (w b)"), bank[5][0:H, :]))
        link(absolute(gv[:, 1:WD + 1, :], gt[:, :, :]))
        link(v.tensor_copy(gv[:, 0, :], gv[:, 2, :]))
        link(v.tensor_copy(gv[:, WD + 1, :], gv[:, WD - 1, :]))
        half = WD // 2

        def weights(col, w0):
            return con[0:H, col + w0:col + w0 + half].unsqueeze(2).to_broadcast([H, half, B])

        for lo, w0 in ((0, 0), (half + 1, half)):
            dst = g4[:, 1, w0:w0 + half, :]
            link(v.tensor_tensor(gt[:, w0:w0 + half, :], gv[:, lo:lo + half, :], weights(C_WLO, w0), ALU.mult))
            link(v.tensor_tensor(dst, gv[:, lo + 1:lo + 1 + half, :], weights(C_WHI, w0), ALU.mult))
            link(v.tensor_tensor(dst, dst, gt[:, w0:w0 + half, :], ALU.add))
        dve.wait_ge(rows_mm, 1)
        link(v.tensor_copy(g4[:, 0].rearrange("h w b -> h (w b)"), bank[4][0:H, :]))
        link(v.tensor_tensor(g4[:, 2], g4[:, 0], g4[:, 1], ALU.subtract))
        link(absolute(g4[:, 2], g4[:, 2]))
        poolw = con[0:H, C_POOLW:C_POOLW + WD].unsqueeze(2).to_broadcast([H, WD, B])
        for k in range(3):
            ins = v.tensor_tensor(g4[:, k], g4[:, k], poolw, ALU.mult)
        link(ins)
        link(v.tensor_reduce(pooled[:, 0:3, :], g4[:, 0:3, :, :].rearrange("h k w b -> h k b w"), AX, ALU.add))
        link(v.tensor_tensor(pooled[:, 3, :], pooled[:, 0, :], pooled[:, 1, :], ALU.add))
        v.tensor_scalar(pooled[:, 3, :], pooled[:, 3, :], 0.5, None, ALU.mult).then_inc(pooled_set, 1)
        dve.wait_ge(scores_mm, 1)
        v.tensor_copy(scores[:, :], bank[5][0:4, 0:B]).then_inc(scores_set, 1)
        dve.wait_ge(hid_mm, 1)
        v.tensor_scalar(hid1[:, :], bank[4][0:32, 0:B], mlpb1[:, 0:1], 0.0, ALU.add, ALU.max).then_inc(hid_set, 1)
        dve.wait_ge(logits_mm, 1)
        link(v.tensor_tensor(lg[:, 0:4], bank[5][0:B, 0:4], mlpb2[:, :], ALU.add))
        link(v.tensor_reduce(lg[:, 13:14], lg[:, 0:4], AX, ALU.max))
        v.tensor_scalar(lg[:, 12:13], lg[:, 13:14], -1.0, None, ALU.mult).then_inc(logits_set, 1)
        dve.wait_ge(exp_set, 1)
        link(v.tensor_reduce(lg[:, 14:15], lg[:, 4:8], AX, ALU.add))
        link(v.reciprocal(lg[:, 15:16], lg[:, 14:15]))
        link(v.tensor_scalar(lg[:, 8:12], lg[:, 4:8], lg[:, 15:16], None, ALU.mult))
        link(v.tensor_scalar(lg[:, 4:5], lg[:, 8:9], lg[:, 9:10], None, ALU.is_lt))
        link(v.tensor_scalar(lg[:, 5:7], lg[:, 10:12], lg[:, 9:10], None, ALU.is_le))
        link(v.tensor_tensor(lg[:, 7:8], lg[:, 5:6], lg[:, 6:7], ALU.mult))
        link(v.tensor_tensor(lg[:, 7:8], lg[:, 7:8], lg[:, 4:5], ALU.mult))
        v.tensor_scalar(diag[:, :], con[0:B, C_IDENT:C_IDENT + B], lg[:, 7:8], None, ALU.mult).then_inc(diag_set, 1)
        dve.wait_ge(mask_mm, 1)
        link(v.tensor_copy(mask[:, :], bank[7][:, 0:B]))
        dve.wait_ge(seq_set, 2 * B)

        def select(t0, t1):
            return v.copy_predicated(seq[:, t0:t1, :], mask[:, :].unsqueeze(1).to_broadcast([P, t1 - t0, B]),
                                     seq_v[:, t0:t1, :])

        select(0, EDGE)
        select(L - EDGE, L).then_inc(select_done, 1)

        dve.wait_ge(init_done, N_INIT)

        def add_output(j, d, ready, landed):
            dve.wait_ge(y_ready, ready)
            dve.wait_ge(tile_in[landed[0]], landed[1])
            kk = j if d == 0 else j * -1 + (NBLK - 1)
            t = tiles[:, bass.ds(kk, 1), :].rearrange("p a c -> p (a c)")
            v.tensor_tensor(t, Y[:, d * C:(d + 1) * C], t, ALU.add).then_inc(y_used, 1)

        def step(base, r, selecting):
            q, s, e, prev = r // TB, r % TB, r % 2, (r - 1) % RING
            turn = base + (r + 1)
            share = (L - 2 * EDGE) // RING
            at = EDGE + r * share
            dve.wait_ge(reset_ready, turn)
            dve.wait_ge(hn_ready, turn)
            v.tensor_tensor_scan(cand[:, e * 2 * COLS:(e + 1) * 2 * COLS], rpair[:, e, :], NX[q][:, s * 2 * COLS:(s + 1) * 2 * COLS], 0.0,
                                 ALU.mult, ALU.add).then_inc(cand_pre, 1)
            if selecting:
                select(at, at + share * 2 // 5)
            dve.wait_ge(cand_ready, turn)
            dve.wait_ge(update_ready, turn)
            if not (isinstance(base, int) and base + r == 0):
                dve.wait_ge(neg_ready, base + r)
            v.tensor_tensor_scan(state[:, r, :], ztrip[:, e, :], state[:, prev, :], 0.0,
                                 ALU.mult, ALU.add).then_inc(state_ready, 1)
            new = state[:, r, :].rearrange("p (n k) -> p n k", k=3)
            hi = state[:, r, :].bitcast(BF16).rearrange("p (n k) -> p n k", k=6)[:, :, 5]
            dve.wait_ge(state_ready, turn)
            v.tensor_tensor(resid[:, e, :], new[:, :, 2], hi, ALU.subtract).then_inc(resid_ready, 1)
            v.tensor_scalar(half_hi[:, e, :], new[:, :, 2], HSCALE, None, ALU.mult).then_inc(half_hi_ready, 1)
            dve.wait_ge(resid_ready, turn)
            v.tensor_tensor(low[:, e, :], resid[:, e, :],
                            resid[:, e, :].bitcast(BF16).rearrange("p (n k) -> p n k", k=2)[:, :, 1],
                            ALU.subtract).then_inc(low_ready, 1)
            dve.wait_ge(half_hi_ready, turn)
            v.scalar_tensor_tensor(out=half_lo[:, e, :], in0=new[:, :, 2], scalar=HSCALE, in1=half_hi[:, e, :],
                                   op0=ALU.mult, op1=ALU.subtract).then_inc(half_lo_ready, 1)
            v.tensor_scalar(new[:, :, 1], new[:, :, 2], -1.0, None, ALU.mult).then_inc(neg_ready, 1)
            if selecting:
                ins = select(at + share * 2 // 5, at + share)
                if r == RING - 1:
                    ins.then_inc(select_rest, 1)

        def body(base, kblk, first, landed):
            for r in range(RING):
                q, s = r // TB, r % TB
                step(base, r, first)
                if s in (3, 5) and not first:
                    add_output(kblk + (q - 2), s // 4, kblk + (q - 1), landed[q])

        body(0, 0, True, None)
        with dve.Fori(1, NBLK // 4) as i:
            body(i * RING, i * 2, False, ((0, i * 32), (1, i * 32)))
        with dve.Fori(NBLK // 4, NBLK // 2) as i:
            body(i * RING, i * 2, False, ((0, 8 * NBLK), (1, 8 * NBLK)))
        for k in (NBLK - 2, NBLK - 1):
            for d in range(2):
                add_output(k, d, k + 1, (k % 2, 8 * NBLK))

    ctx.close()


def kernel(x, L0_conv_ln_gamma, L0_conv_ln_beta, L0_conv_mlp_w1, L0_conv_mlp_b1, L0_conv_mlp_w2, L0_conv_mlp_b2,
           L0_conv_in_w, L0_conv_in_b, L0_conv_gru_wih_f, L0_conv_gru_whh_f, L0_conv_gru_bih_f, L0_conv_gru_bhh_f,
           L0_conv_gru_wih_b, L0_conv_gru_whh_b, L0_conv_gru_bih_b, L0_conv_gru_bhh_b, L0_conv_out_w, L0_conv_out_b):
    import numpy as np
    import concourse.bacc as bacc
    from concourse.bass_utils import run_bass_kernel_spmd

    def both(f, b):
        return np.stack([np.asarray(f), np.asarray(b)])

    def turned(a):
        return np.ascontiguousarray(np.swapaxes(np.asarray(a), -1, -2))

    def column(a):
        return np.asarray(a)[:, None]

    arrays = {
        "x": x, "gamma": column(L0_conv_ln_gamma), "beta": column(L0_conv_ln_beta),
        "w1t": turned(L0_conv_mlp_w1), "b1": column(L0_conv_mlp_b1), "w2t": turned(L0_conv_mlp_w2), "b2": np.asarray(L0_conv_mlp_b2)[None, :],
        "in_w": L0_conv_in_w, "in_b": turned(np.asarray(L0_conv_in_b).reshape(DI // P, P)),
        "wiht": turned(both(L0_conv_gru_wih_f, L0_conv_gru_wih_b)),
        "whht": turned(both(L0_conv_gru_whh_f, L0_conv_gru_whh_b)),
        "bih": both(L0_conv_gru_bih_f, L0_conv_gru_bih_b).reshape(2, 3, HID).transpose(2, 0, 1),
        "bhh": both(L0_conv_gru_bhh_f, L0_conv_gru_bhh_b).reshape(2, 3, HID).transpose(2, 0, 1),
        "outwt": turned(L0_conv_out_w), "out_b": column(L0_conv_out_b), "consts": shape_constants(),
    }
    nc = bacc.Bacc("TRN2", target_bir_lowering=False, num_devices=1)
    fed, aps = {}, []
    for name, a in arrays.items():
        a = np.ascontiguousarray(a)
        fed[f"in_{name}"] = a
        aps.append(nc.dram_tensor(f"in_{name}", a.shape, mybir.dt.from_np(a.dtype), kind="ExternalInput").ap())
    aps.append(nc.dram_tensor("out", (B, H, WD, C), F32, kind="ExternalOutput").ap())
    build(nc, *aps)
    got = run_bass_kernel_spmd(nc, [fed], core_ids=[0])
    return got.results[0]["out"]
```

```python
from contextlib import ExitStack

import concourse.bass as bass
from concourse import mybir

P = 128
B, H, WD, C = 16, 32, 32, 128
L = H * WD
DI = 2 * C
HID = 128
TB = 8
NBLK = L // TB
RING = 2 * TB
COLS = 2 * B
TPP = L // P
EDGE = 4 * TB
SLOTS = 4
JA = 2
K = 2.0 ** 12
BIG = 1.5 * 2.0 ** 12 * K
NORM_MIN = 2.0 ** 5
TOP = 2.0 ** 14
EPS = 1e-5

F32 = mybir.dt.float32
BF16 = mybir.dt.bfloat16
F16 = mybir.dt.float16
I32 = mybir.dt.int32
ALU = mybir.AluOpType
ACT = mybir.ActivationFunctionType
AX = mybir.AxisListType.X
G_R, G_Z, G_N, G_HN = range(4)

C_IDENT = 0
C_SELECT = C_IDENT + P
C_MEAN = C_SELECT + P
C_DIFF = C_MEAN + H
C_RESIZE = C_DIFF + H
C_POOLH = C_RESIZE + H
C_WLO = C_POOLH + 16
C_WHI = C_WLO + WD
C_POOLW = C_WHI + WD
C_ONES = C_POOLW + WD
C_IND = C_ONES + P
C_END = C_IND + 2 * P


def shape_constants():
    import numpy as np

    t = np.zeros((P, C_END), np.float32)
    t[:, C_IDENT:C_IDENT + P] = np.eye(P)
    ppr = P // H
    for p in range(P):
        t[p, C_SELECT + (p % ppr) * H + p // ppr] = 1.0 / C
    t[:, C_MEAN:C_MEAN + H] = 1.0 / C
    for i in range(1, H - 1):
        t[i + 1, C_DIFF + i] += 1.0
        t[i - 1, C_DIFF + i] -= 1.0
    for i in range(H):
        src = min(max((i + 0.5) * (H + 2) / H - 0.5, 0.0), H + 1)
        lo = int(np.floor(src))
        w = src - lo
        for k, v in ((lo, 1.0 - w), (min(lo + 1, H + 1), w)):
            row = k - 1
            row = -row if row < 0 else (2 * (H - 1) - row if row > H - 1 else row)
            t[row, C_RESIZE + i] += v
        t[:, C_WLO + i] = 1.0 - w
        t[:, C_WHI + i] = w
        edge = 2.0 if i in (0, H - 1) else 3.0
        for k in range(4):
            t[i, C_POOLH + 4 * k + k] = edge / (9.0 * H * WD)
        t[:, C_POOLW + i] = edge
    t[:, C_ONES:C_ONES + P] = 1.0
    ind = t[:, C_IND:C_IND + 2 * P].reshape(P, TB, 2, B)
    for part in range(3):
        for d in range(2):
            ind[3 * d + part, :, d, :] = 1.0
    t[:, C_IND:C_IND + 2 * P] = ind.reshape(P, 2 * P)
    return t


def build(nc, x, gamma, beta, w1t, b1, w2t, b2, in_w, in_b, wiht, whht, bih, bhh, outwt, out_b, consts, out):
    ctx = ExitStack()

    def sb(name, shape, dt=F32):
        return ctx.enter_context(nc.sbuf_tensor(name, shape, dt))

    def sem(name):
        return ctx.enter_context(nc.semaphore(name))

    seq = sb("seq", [P, L, B])
    big = sb("big", [P, L * B])
    seq_v = big[:, :].rearrange("c (t b) -> c t b", b=B)
    tiles = big[:, :].rearrange("p (k c) -> p k c", c=C)
    xin = sb("xin", [P, SLOTS, TPP, C])
    stats = sb("stats", [P, SLOTS, TPP, 6])
    moments = sb("moments", [P, SLOTS, TPP, 2])
    std = sb("std", [P, SLOTS, TPP])
    rstd = sb("rstd", [P, SLOTS, TPP])
    shift = sb("shift", [P, SLOTS, TPP])
    gamma_row = sb("gamma_row", [P, C])
    weighted = sb("weighted", [P, TPP, C])
    gray_tok = sb("gray_tok", [P, B, TPP])
    beta_mean = sb("beta_mean", [H, 1])
    gb = sb("gb", [P, 2])
    eps = sb("eps", [P, 1])
    table = sb("table", [P, 1])
    con = sb("con", [P, C_END])
    ind = sb("ind", [6, 2 * P], BF16)
    inw = sb("inw", [P, DI // P, C])
    inb = sb("inb", [P, DI // P])
    wih = sb("wih", [P, 2, DI // P, 3 * HID])
    whh = sb("whh", [P, 2, 3 * HID])
    wsplit = sb("wsplit", [P, 2, 2, 3 * HID], F16)
    square = sb("square", [P, 2 * 3 * HID])
    sums = sb("sums", [P, 1])
    norm = sb("norm", [P, 2])
    scale = sb("scale", [P, 3])
    sk = sb("sk", [P, 1])
    usual = sb("usual", [1, 1], I32)
    wcomb = sb("wcomb", [P, 2, 3 * HID])
    outw = sb("outw", [P, 2, C])
    bfold = sb("bfold", [P, 2, 3])
    bih_col = sb("bih_col", [P, 2, 3])
    bhh_col = sb("bhh_col", [P, 2, 3])
    bias_col = sb("bias_col", [P, 9])
    bias_bf = sb("bias_bf", [P, 3, 9], BF16)
    bias_part = sb("bias_part", [P, 9 * 3])
    bias6 = sb("bias6", [6, 4 * HID], BF16)
    obias = sb("obias", [3, C], BF16)
    ones3 = sb("ones3", [3, P], BF16)
    mlp1 = sb("mlp1", [4, 32])
    mlpb1 = sb("mlpb1", [32, 1])
    mlp2 = sb("mlp2", [32, 4])
    mlpb2 = sb("mlpb2", [B, 4])
    g4 = xin[0:H, 0:2].rearrange("h q j c -> h (q j c)").rearrange("h (k w b) -> h k w b", k=4, b=B)
    spare = xin[0:H, 2:4].rearrange("h q j c -> h (q j c)").rearrange("h (w b) -> h w b", b=B)
    gray, gv, gh = spare[:, 0:WD + 2], spare[:, WD + 2:2 * WD + 4], spare[:, 2 * WD + 4:3 * WD + 4]
    gt = sb("gt", [H, WD, B])
    pooled = sb("pooled", [H, 4, B])
    scores = sb("scores", [4, B])
    hid1 = sb("hid1", [32, B])
    lg = sb("lg", [B, 16])
    diag = sb("diag", [B, B])
    mask = sb("mask", [P, B], I32)
    rev = sb("rev", [P, 2, TB, B])
    hist = sb("hist", [P, 2, 2, B, TB])
    state = sb("state", [P, RING, 4 * COLS])
    rec = sb("rec", [P, 2, 4 * COLS])
    signs = sb("signs", [P, 2 * COLS])
    h_hi = sb("h_hi", [P, 2, COLS], F16)
    h_lo = sb("h_lo", [P, 2, COLS], F16)
    rpair = sb("rpair", [P, 2, 2 * COLS])
    zquad = sb("zquad", [P, 2, 4 * COLS])

    bank = [ctx.enter_context(nc.psum_tensor(f"bank{i}", [P, 512], F32)) for i in range(8)]
    R, Z, NX, Y = bank[0:2], bank[2:4], bank[4:6], bank[6]
    cand = bank[7]

    w_in = sem("w_in")
    first_in = sem("first_in")
    x_in = [sem(f"x_in{q}") for q in range(SLOTS)]
    stats_set = sem("stats_set")
    moments_set = sem("moments_set")
    std_set = sem("std_set")
    rstd_set = sem("rstd_set")
    shift_set = sem("shift_set")
    xhat_act = sem("xhat_act")
    xhat_pool = sem("xhat_pool")
    gray_sum = sem("gray_sum")
    select_rest = sem("select_rest")
    fold_set = sem("fold_set")
    link_g = sem("link_g")
    xT_set = sem("xT_set")
    seq_set = sem("seq_set")
    w_mm = sem("w_mm")
    link_v = sem("link_v")
    bias_split = sem("bias_split")
    bias_mm = sem("bias_mm")
    bias_rows = sem("bias_rows")
    cast_set = sem("cast_set")
    weights_set = sem("weights_set")
    gray_mm = sem("gray_mm")
    gray_set = sem("gray_set")
    diff_mm = sem("diff_mm")
    gradh_set = sem("gradh_set")
    rows_mm = sem("rows_mm")
    pooled_set = sem("pooled_set")
    scores_mm = sem("scores_mm")
    scores_set = sem("scores_set")
    hid_mm = sem("hid_mm")
    hid_set = sem("hid_set")
    logits_mm = sem("logits_mm")
    logits_set = sem("logits_set")
    exp_set = sem("exp_set")
    diag_set = sem("diag_set")
    mask_mm = sem("mask_mm")
    select_done = sem("select_done")
    init_done = sem("init_done")
    reset_pre = [sem(f"reset_pre{d}") for d in range(2)]
    hn_ready = [sem(f"hn_ready{d}") for d in range(2)]
    update_pre = [sem(f"update_pre{d}") for d in range(2)]
    reset_ready = [sem(f"reset_ready{d}") for d in range(2)]
    update_ready = [sem(f"update_ready{d}") for d in range(2)]
    cand_pre = [sem(f"cand_pre{d}") for d in range(2)]
    cand_ready = [sem(f"cand_ready{d}") for d in range(2)]
    state_ready = [sem(f"state_ready{d}") for d in range(2)]
    hi_ready = [sem(f"hi_ready{d}") for d in range(2)]
    lo_ready = [sem(f"lo_ready{d}") for d in range(2)]
    rec_ready = [sem(f"rec_ready{d}") for d in range(2)]
    square_set = sem("square_set")
    norm_mm = sem("norm_mm")
    norm_set = sem("norm_set")
    scale_set = sem("scale_set")
    hist_ready = sem("hist_ready")
    rev_ready = sem("rev_ready")
    images_counted = sem("images_counted")
    tokens_counted = sem("tokens_counted")
    blocks_counted = sem("blocks_counted")
    y_ready = sem("y_ready")
    y_used = sem("y_used")
    tile_in0 = sem("tile_in0")
    tile_in1 = sem("tile_in1")
    out_done = sem("out_done")
    tile_in = (tile_in0, tile_in1)

    x_tok = x.rearrange("b h w c -> b (h w) c")
    out_tok = out.rearrange("b h w c -> b (h w) c")
    x_part = x_tok.rearrange("b (p j) c -> b p (j c)", j=TPP)

    N_PARAM = 15
    N_FIRST = 4

    def ahead(rnd, q, o):
        return rnd + (q + o) // SLOTS, (q + o) % SLOTS, rnd * SLOTS + (q + o + 1)

    block = ctx.enter_context(nc.Block())

    @block.sync
    def _(sp):
        def load_image(rnd, q, wait):
            b = rnd * SLOTS + q
            if wait:
                sp.wait_ge(gray_sum, b + (1 - SLOTS))
                sp.wait_ge(xT_set, b * 2 + (2 - 2 * SLOTS))
            sp.dma_start(xin[:, q].rearrange("p j c -> p (j c)"),
                         x_part[bass.ds(b, 1)].rearrange("a p n -> (a p) n") if not isinstance(b, int) else x_part[b]
                         ).then_inc(x_in[q], 16)

        load_image(0, 0, False)
        load_image(0, 1, False)
        for dst, src in ((con[:, :], consts), (gb[:, 0:1], gamma), (gb[:, 1:2], beta),
                         (gamma_row[:, :], gamma.rearrange("c a -> a c").to_broadcast((P, C)))):
            sp.dma_start(dst, src).then_inc(first_in, 16)
        load_image(0, 2, False)
        load_image(0, 3, False)
        params = (
            (inw[:, :, :], in_w.rearrange("(k p) c -> p k c", p=P)),
            (inb[:, :], in_b),
            (wih[:, 0], wiht[0].rearrange("(k p) m -> p k m", p=P)),
            (wih[:, 1], wiht[1].rearrange("(k p) m -> p k m", p=P)),
            (whh[:, 0], whht[0]), (whh[:, 1], whht[1]),
            (outw[:, 0], outwt[0:HID]), (outw[:, 1], outwt[HID:2 * HID]),
            (mlp1[:, :], w1t), (mlpb1[:, :], b1), (mlp2[:, :], w2t),
            (mlpb2[:, :], b2.to_broadcast((B, 4))),
            (bih_col[:, :, :], bih), (bhh_col[:, :, :], bhh), (bias_col[:, 8:9], out_b),
        )
        assert len(params) == N_PARAM
        for q in range(SLOTS):
            load_image(1, q, True)
            for dst, src in params[q * 4:q * 4 + 4]:
                sp.dma_start(dst, src).then_inc(w_in, 16)
        with sp.Fori(2, B // SLOTS) as i:
            for q in range(SLOTS):
                load_image(i, q, True)
        sp.wait_ge(select_done, 1)

        def tile_rows(t, k):
            return t[:, bass.ds(k * TB, TB), :]

        def load_tiles(k, q, wait):
            if wait is not None:
                sp.wait_ge(y_used, wait)
            for kk in (k, k * -1 + (NBLK - 1)):
                sp.dma_start(tiles[:, bass.ds(kk, 1), :].rearrange("p a c -> p (a c)"),
                             tile_rows(x_tok, kk)).then_inc(tile_in[q], 16)

        load_tiles(0, 0, None)
        load_tiles(1, 1, None)
        sp.wait_ge(select_rest, 1)
        with sp.Fori(1, NBLK // 4) as i:
            for q in range(2):
                load_tiles(i * 2 + q, q, i * 4 + (2 * q - 2))
        with sp.Fori(NBLK // 4, NBLK // 2) as i:
            for q in range(2):
                for d in range(2):
                    k = i * 2 + q
                    kk = k if d == 0 else k * -1 + (NBLK - 1)
                    sp.wait_ge(y_used, i * 4 + (2 * q + d + 1))
                    sp.dma_start(tile_rows(out_tok, kk),
                                 tiles[:, bass.ds(kk, 1), :].rearrange("p a c -> p (a c)")).then_inc(out_done, 16)
        sp.wait_ge(out_done, 16 * NBLK)

    N_INIT = 15

    @block.gpsimd
    def _(g):
        g.memset(rpair[:, :, :], 0.0).then_inc(init_done, 1)
        for e in range(2):
            quad = zquad[:, e, :].rearrange("p (n k) -> p n k", k=4)
            g.memset(quad[:, :, 0], 0.0).then_inc(init_done, 1)
            g.memset(quad[:, :, 1], K).then_inc(init_done, 1)
            g.memset(quad[:, :, 3], -1.0).then_inc(init_done, 1)
            rows = rec[:, e, :].rearrange("p (n k) -> p n k", k=4)
            g.memset(rows[:, :, 1:3], 0.0).then_inc(init_done, 1)
            g.memset(rows[:, :, 3], -BIG).then_inc(init_done, 1)
        pairs = signs[:, :].rearrange("p (n k) -> p n k", k=2)
        g.memset(pairs[:, :, 0], -1.0).then_inc(init_done, 1)
        g.memset(pairs[:, :, 1], 1.0).then_inc(init_done, 1)
        g.memset(h_hi[:, :, :], 0.0).then_inc(init_done, 1)
        g.memset(h_lo[:, :, :], 0.0).then_inc(init_done, 1)
        def normalise(rnd, q):
            turn = ahead(rnd, q, 0)[2]
            g.wait_ge(shift_set, turn)
            g.sem_inc(tokens_counted, 1)
            for j in range(JA, TPP):
                ins = g.tensor_scalar(xin[:, q, j, :], xin[:, q, j, :], rstd[:, q, j:j + 1], shift[:, q, j:j + 1],
                                      ALU.mult, ALU.add)
            ins.then_inc(xhat_pool, 1)

        g.wait_ge(first_in, 16 * N_FIRST)
        for q in range(SLOTS):
            normalise(0, q)
        with g.Fori(1, B // SLOTS) as i:
            for q in range(SLOTS):
                normalise(i, q)

        links = [0]

        def link(ins):
            links[0] += 1
            ins.then_inc(link_g, 1)
            g.wait_ge(link_g, links[0])

        g.wait_ge(w_in, 16 * N_PARAM)
        g.wait_ge(fold_set, 1)
        total = bias_col[:, 0:8].rearrange("p (g d) -> p d g", d=2)
        link(g.tensor_tensor(total[:, :, 0:3], bfold[:, :, :], bih_col[:, :, :], ALU.add))
        link(g.tensor_tensor(total[:, :, 0:2], total[:, :, 0:2], bhh_col[:, :, 0:2], ALU.add))
        link(g.tensor_copy(total[:, :, 3], bhh_col[:, :, 2]))
        g.wait_ge(scale_set, 1)
        link(g.tensor_scalar(bias_col[:, 0:8], bias_col[:, 0:8], sk[:, 0:1], None, ALU.mult))
        for k in range(3):
            link(g.tensor_copy(bias_bf[:, k, :], bias_col[:, :]))
            if k < 2:
                link(g.tensor_tensor(bias_col[:, :], bias_col[:, :], bias_bf[:, k, :], ALU.subtract))
        g.tensor_copy(bias_part[:, :].rearrange("p (n k) -> p k n", k=3), bias_bf[:, :, :]).then_inc(bias_split, 1)
        g.tensor_copy(ind[:, :], con[0:6, C_IND:C_IND + 2 * P]).then_inc(cast_set, 1)
        link(g.tensor_scalar(outw[:, :, :], outw[:, :, :], 1.0 / K, None, ALU.mult))
        w_all = whh[:, :, :].rearrange("p d n -> p (d n)")
        parts = [wsplit[:, k].rearrange("p d n -> p (d n)") for k in range(2)]
        g.wait_ge(square_set, 1)
        link(g.tensor_scalar(w_all, w_all, scale[:, 2:3], None, ALU.mult))
        link(g.tensor_copy(parts[0], w_all))
        g.tensor_tensor(parts[1], w_all, parts[0], ALU.subtract).then_inc(weights_set, 1)

        def reorder(k, q, wait):
            for d in range(2):
                g.wait_ge(state_ready[d], (k + 1) * TB)
            if wait:
                g.wait_ge(y_ready, k - 1)
            g.sem_inc(blocks_counted, 1)
            for d in range(2):
                h = state[:, q * TB:(q + 1) * TB, :].rearrange("p s (d b k) -> p s d b k", d=2, k=4)[:, :, d, :, 2]
                if d == 0:
                    ins = g.tensor_copy(hist[:, q, d], h.rearrange("p s b -> p b s"))
                else:
                    for s in range(TB):
                        ins = g.tensor_copy(hist[:, q, d, :, TB - 1 - s], h[:, s, :])
            ins.then_inc(hist_ready, 1)

        def reverse(k, q):
            for s in range(TB):
                ins = g.tensor_copy(rev[:, q, s, :], seq[:, bass.ds(k * -TB + (L - 1 - s), 1), :].rearrange("c a b -> c (a b)"))
            ins.then_inc(rev_ready, 1)

        g.wait_ge(select_done, 1)
        for q in range(2):
            reverse(q, q)
        for q in range(2):
            reorder(q, q, False)
            reverse(q + 2, q)
        g.wait_ge(select_rest, 1)
        with g.Fori(1, NBLK // 2 - 1) as i:
            for q in range(2):
                reorder(i * 2 + q, q, True)
                reverse(i * 2 + (q + 2), q)
        for q in range(2):
            reorder(NBLK - 2 + q, q, True)

    @block.scalar
    def _(act):
        def deviation(rnd, q, o):
            _, qo, turn = ahead(rnd, q, o)
            act.wait_ge(moments_set, turn)
            act.activation(std[:, qo, :], moments[:, qo, :, 1], ACT.Sqrt, bias=eps[:, 0:1]).then_inc(std_set, 1)

        def normalise(rnd, q):
            act.wait_ge(shift_set, ahead(rnd, q, 0)[2])
            for j in range(JA):
                ins = act.activation(xin[:, q, j, :], xin[:, q, j, :], ACT.Identity,
                                     bias=shift[:, q, j:j + 1], scale=rstd[:, q, j:j + 1])
            ins.then_inc(xhat_act, 1)

        def evacuate(rnd, q, halves=(0, 1)):
            _, q1, turn = ahead(rnd, q, -1)
            for half in halves:
                act.wait_ge(xT_set, turn * 2 + (half - 1))
                src = bank[2 * (q1 % 2) + half]
                dst = seq[:, :, :].rearrange("c (p j) b -> c j p b", j=TPP)[:, 4 * half:4 * half + 4, :, bass.ds(turn - 1, 1)]
                act.activation(dst.rearrange("c j p b -> c j (p b)"), src[:, :].rearrange("c (j p) -> c j p", j=4),
                               ACT.Identity, bias=gb[:, 1:2], scale=gb[:, 0:1])
                dst = seq_v.rearrange("c (m j h) b -> c j h m b", m=WD // TPP, j=TPP)[
                    :, 4 * half:4 * half + 4, :, :, bass.ds(turn - 1, 1)].rearrange("c j h m b -> c j h (m b)")
                act.activation(dst, src[:, :].rearrange("c (j h m) -> c j h m", j=4, m=WD // TPP),
                               ACT.Identity, bias=gb[:, 1:2], scale=gb[:, 0:1]).then_inc(seq_set, 1)

        def image(rnd, q, first=False, last=False):
            normalise(rnd, q)
            if not (first and q == 0):
                evacuate(rnd, q, (0,))
            if not (last and q == SLOTS - 1):
                deviation(rnd, q, 1)
            if not (first and q == 0):
                evacuate(rnd, q, (1,))

        act.wait_ge(cast_set, 1)
        act.activation(table[:, :], eps[:, :], ACT.Sqrt)
        deviation(0, 0, 0)
        act.wait_ge(first_in, 16 * N_FIRST)
        for q in range(SLOTS):
            image(0, q, first=True)
        with act.Fori(1, B // SLOTS - 1) as i:
            for q in range(SLOTS):
                image(i, q)
        for q in range(SLOTS):
            image(B // SLOTS - 1, q, last=True)
        evacuate(B // SLOTS, 0)
        act.wait_ge(w_mm, 1)
        for d in range(2):
            ins = act.copy(bfold[:, d, :], bank[6 + d][:, 3 * HID:3 * HID + 3])
        ins.then_inc(fold_set, 1)
        act.activation(square[:, :], whh[:, :, :].rearrange("p d n -> p (d n)"), ACT.Square,
                       accum_out=sums[:, 0:1]).then_inc(square_set, 1)
        act.wait_ge(norm_mm, 1)
        act.activation(norm[:, 0:1], bank[7][:, 3 * HID + 3:3 * HID + 4], ACT.Sqrt).then_inc(norm_set, 1)
        act.wait_ge(scale_set, 1)
        for d in range(2):
            act.activation(wcomb[:, d, :], bank[6 + d][:, 0:3 * HID], ACT.Identity,
                           scale=sk[:, 0:1]).then_inc(fold_set, 1)
        act.wait_ge(bias_mm, 1)
        act.copy(bias6[:, :], bank[0][0:6, :])
        act.copy(obias[:, :], bank[1][0:3, 0:C]).then_inc(bias_rows, 1)

        act.wait_ge(logits_set, 1)
        act.activation(lg[:, 4:8], lg[:, 0:4], ACT.Exp, bias=lg[:, 12:13]).then_inc(exp_set, 1)
        act.activation(table[:, :], eps[:, :], ACT.Sigmoid)

        act.wait_ge(init_done, N_INIT)

        def body(base, inverse, negative):
            for r in range(RING):
                q, s, e = r // TB, r % TB, r % 2
                turn = base + (r + 1)
                for d in range(2):
                    at = s * COLS + d * B
                    act.wait_ge(reset_pre[d], turn)
                    act.activation(rpair[:, e, 2 * B * d:2 * B * (d + 1)].rearrange("p (n k) -> p n k", k=2)[:, :, 1],
                                   R[q][:, at:at + B], ACT.Sigmoid, scale=inverse).then_inc(reset_ready[d], 1)
                    act.wait_ge(update_pre[d], turn)
                    act.activation(zquad[:, e, 4 * B * d:4 * B * (d + 1)].rearrange("p (n k) -> p n k", k=4)[:, :, 2],
                                   Z[q][:, at:at + B], ACT.Sigmoid, scale=negative).then_inc(update_ready[d], 1)
                    act.wait_ge(cand_pre[d], turn)
                    act.activation(rec[:, e, 4 * B * d:4 * B * (d + 1)].rearrange("p (n k) -> p n k", k=4)[:, :, 0],
                                   cand[:, (2 * e + d) * 2 * B:(2 * e + d + 1) * 2 * B].rearrange("p (n k) -> p n k", k=2)[:, :, 1],
                                   ACT.Tanh, scale=inverse).then_inc(cand_ready[d], 1)

        def recurrence(inverse, negative):
            body(0, inverse, negative)
            with act.Fori(1, L // RING // 2) as i:
                body(i * (2 * RING) - RING, inverse, negative)
                body(i * (2 * RING), inverse, negative)
            body(L - RING, inverse, negative)

        is_usual = act.value_load(usual[0:1, 0:1], min_val=0, max_val=1)
        with act.If(is_usual == 1):
            recurrence(NORM_MIN / (TOP * K), -NORM_MIN / (TOP * K))
        with act.Else():
            recurrence(scale[:, 0:1], scale[:, 1:2])

    @block.tensor
    def _(pe):
        identity = con[:, C_IDENT:C_IDENT + P]

        def transposes(rnd, q, first=False):
            turn = ahead(rnd, q, 0)[2]
            for half in range(2):
                if half == 0:
                    pe.wait_ge(xhat_pool, turn)
                    pe.wait_ge(xhat_act, turn)
                if not (first and q < 2):
                    pe.wait_ge(seq_set, turn * 2 + (half - 5))
                for j in range(4):
                    ins = nc.tensor.transpose(bank[2 * (q % 2) + half][:, j * P:(j + 1) * P],
                                              xin[:, q, 4 * half + j, :], identity)
                ins.then_inc(xT_set, 1)

        pe.wait_ge(first_in, 16 * N_FIRST)
        for q in range(SLOTS):
            transposes(0, q, True)
        for q in range(SLOTS):
            transposes(1, q)
        pe.wait_ge(w_in, 16 * N_PARAM)
        for d in range(2):
            for k in range(DI // P):
                nc.tensor.matmul(bank[6 + d][:, 0:3 * HID], inw[:, k, :], wih[:, d, k, :],
                                 start=(k == 0), stop=(k == DI // P - 1))
            for g in range(3):
                for k in range(DI // P):
                    ins = nc.tensor.matmul(bank[6 + d][:, 3 * HID + g:3 * HID + g + 1],
                                           wih[:, d, k, g * HID:(g + 1) * HID], inb[:, k:k + 1],
                                           start=False, stop=(k == DI // P - 1), skip_group_check=True)
        ins.then_inc(w_mm, 1)
        with pe.Fori(2, B // SLOTS) as i:
            for q in range(SLOTS):
                transposes(i, q)

        pe.wait_ge(gray_sum, B)
        for k in range(P // H):
            nc.tensor.matmul(bank[4][0:H, k * P:(k + 1) * P], con[:, C_SELECT + k * H:C_SELECT + (k + 1) * H],
                             gray_tok[:, :, :].rearrange("p b j -> p (b j)"), start=True, stop=True)
        nc.tensor.matmul(bank[5][0:H, 0:1], con[:, C_MEAN:C_MEAN + H], gb[:, 1:2], start=True, stop=True).then_inc(gray_mm, 1)
        pe.wait_ge(square_set, 1)
        nc.tensor.matmul(bank[7][:, 3 * HID + 3:3 * HID + 4], con[:, C_ONES:C_ONES + P], sums[:, :],
                         start=False, stop=True, skip_group_check=True).then_inc(norm_mm, 1)
        pe.wait_ge(gray_set, 1)
        nc.tensor.matmul(bank[5][0:H, :], con[0:H, C_DIFF:C_DIFF + H],
                         gray[:, 1:WD + 1, :].rearrange("h w b -> h (w b)"), start=True, stop=True).then_inc(diff_mm, 1)
        pe.wait_ge(gradh_set, 1)
        nc.tensor.matmul(bank[4][0:H, :], con[0:H, C_RESIZE:C_RESIZE + H],
                         gh[:, :, :].rearrange("h w b -> h (w b)"), start=True, stop=True).then_inc(rows_mm, 1)
        pe.wait_ge(bias_split, 1)
        pe.wait_ge(seq_set, 2 * B)
        for g in range(4):
            nc.tensor.transpose(bank[0][0:6, g * HID:(g + 1) * HID], bias_part[:, 6 * g:6 * g + 6], identity)
        nc.tensor.transpose(bank[1][0:3, 0:C], bias_part[:, 24:27], identity).then_inc(bias_mm, 1)
        pe.wait_ge(pooled_set, 1)
        for k, at in enumerate((0, 1, 3, 2)):
            ins = nc.tensor.matmul(bank[5][0:4, 0:B], con[0:H, C_POOLH + 4 * k:C_POOLH + 4 * k + 4],
                                   pooled[:, at, :], start=(k == 0), stop=(k == 3))
        ins.then_inc(scores_mm, 1)
        pe.wait_ge(scores_set, 1)
        nc.tensor.matmul(bank[4][0:32, 0:B], mlp1[:, :], scores[:, :], start=True, stop=True).then_inc(hid_mm, 1)
        pe.wait_ge(hid_set, 1)
        nc.tensor.matmul(bank[5][0:B, 0:4], hid1[:, :], mlp2[:, :], start=True, stop=True).then_inc(logits_mm, 1)
        pe.wait_ge(diag_set, 1)
        pe.wait_ge(fold_set, 3)
        nc.tensor.matmul(bank[7][:, 0:B], con[0:B, C_ONES:C_ONES + P], diag[:, :], start=True, stop=True).then_inc(mask_mm, 1)

        def mm(o, w, m, start=False):
            return nc.tensor.matmul(o, w, m, start=start, stop=True, skip_group_check=True)

        def nx(q):
            return NX[q][:, :].rearrange("p (s d b k) -> p s d b k", s=TB, d=2, k=2)

        def gate(banks, q):
            return banks[q][:, 0:TB * COLS].rearrange("p (s d b) -> p s d b", s=TB, d=2)

        def fill_bias(q, which):
            if which in (G_R, G_Z):
                bk = (R if which == G_R else Z)[q]
                return mm(bk[:, 0:2 * TB * B], bias6[:, which * HID:(which + 1) * HID],
                          ind[:, :], start=True)
            k = 0 if which == G_HN else 1
            return mm(NX[q][:, k::2], bias6[:, which * HID:(which + 1) * HID],
                      ind[:, :], start=(which == G_HN))

        def fill_input(q, kblk, g, d):
            src = seq[:, bass.ds(kblk * TB, TB), :] if d == 0 else rev[:, q]
            w = wcomb[:, d, g * HID:(g + 1) * HID]
            if g == G_N:
                return mm(nx(q)[:, :, d, :, 1], w, src)
            return mm(gate(R if g == G_R else Z, q)[:, :, d, :], w, src)

        FILL_BIAS = [None, G_R, G_Z, G_HN, G_N, None, None, None]
        FILL_INPUT = [None, (G_R, 0), (G_Z, 0), (G_R, 1), (G_N, 0), (G_Z, 1), (G_N, 1), None]
        FIRST_BACKWARD = 3

        def project(q, d):
            return mm(Y[:, d * C:(d + 1) * C], hist[:, q, d].rearrange("p b s -> p (b s)"), outw[:, d, :],
                      start=(d == 0))

        def output_bias():
            mm(Y[:, 0:C], ones3[:, :], obias[:, :])

        def step(base, r, d):
            q, s, e = r // TB, r % TB, r % 2
            hi = h_hi[:, 1 - e, d * B:(d + 1) * B]
            lo = h_lo[:, 1 - e, d * B:(d + 1) * B]
            out_of = {G_R: gate(R, q)[:, s, d, :], G_Z: gate(Z, q)[:, s, d, :], G_N: nx(q)[:, s, d, :, 0]}

            def run(g, parts):
                for k, h in parts:
                    ins = mm(out_of[g], wsplit[:, k, d, g * HID:(g + 1) * HID], h)
                return ins

            if not (isinstance(base, int) and base + r == 0):
                pe.wait_ge(hi_ready[d], base + r)
            o, others = 1 - d, base + (r + d)
            alone = isinstance(base, int) and base + r + d == 0
            if not alone:
                pe.wait_ge(reset_ready[o], others)
            run(G_R, ((0, hi), (1, hi)))
            if not (isinstance(base, int) and base + r == 0):
                pe.wait_ge(lo_ready[d], base + r)
            run(G_R, ((0, lo),)).then_inc(reset_pre[d], 1)
            if not alone:
                pe.wait_ge(cand_pre[o], others)
            run(G_N, ((0, hi), (1, hi), (0, lo))).then_inc(hn_ready[d], 1)
            if not alone:
                pe.wait_ge(update_ready[o], others)
            run(G_Z, ((0, hi), (1, hi), (0, lo))).then_inc(update_pre[d], 1)

        def body(base, kblk, first=False, last=False):
            for r in range(RING):
                q, s = r // TB, r % TB
                filling = not (last and q == 1)
                step(base, r, 0)
                if s == 0 and not first:
                    output_bias()
                if filling and FILL_BIAS[s] is not None:
                    fill_bias(1 - q, FILL_BIAS[s])
                step(base, r, 1)
                if filling and s == FIRST_BACKWARD:
                    pe.wait_ge(rev_ready, kblk + (q + 2))
                if filling and FILL_INPUT[s] is not None:
                    fill_input(1 - q, kblk + (q + 1), *FILL_INPUT[s])
                if s == TB - 1 and not (first and q == 0):
                    if not (first and q == 1):
                        pe.wait_ge(y_used, (kblk + (q - 1)) * 2)
                    pe.wait_ge(hist_ready, kblk + q)
                    project(1 - q, 0)
                if s == 0 and not first:
                    project(q, 1).then_inc(y_ready, 1)

        pe.wait_ge(bias_rows, 1)
        pe.wait_ge(cast_set, 2)
        pe.wait_ge(weights_set, 1)
        pe.wait_ge(init_done, N_INIT)
        for g in (G_R, G_Z, G_HN, G_N):
            fill_bias(0, g)
        pe.wait_ge(select_done, 1)
        for g in (G_R, G_N, G_Z):
            fill_input(0, 0, g, 0)
        pe.wait_ge(rev_ready, 1)
        for g in (G_R, G_N, G_Z):
            fill_input(0, 0, g, 1)
        body(0, 0, first=True)
        pe.wait_ge(select_rest, 1)
        with pe.Fori(1, L // RING // 2) as i:
            body(i * (2 * RING) - RING, i * 4 - 2)
            body(i * (2 * RING), i * 4)
        body(L - RING, NBLK - 2, last=True)
        output_bias()
        project(0, 1).then_inc(y_ready, 1)
        pe.wait_ge(y_used, 2 * (NBLK - 1))
        pe.wait_ge(hist_ready, NBLK)
        project(1, 0)
        output_bias()
        project(1, 1).then_inc(y_ready, 1)

    @block.vector
    def _(dve):
        v = nc.vector
        links = [0]

        def link(ins):
            links[0] += 1
            ins.then_inc(link_v, 1)
            dve.wait_ge(link_v, links[0])

        link(v.memset(ones3[:, :], 1.0))
        v.memset(eps[:, :], EPS).then_inc(cast_set, 1)

        def statistics(rnd, q, o):
            r1, q1, turn = ahead(rnd, q, o)
            dve.wait_ge(x_in[q1], r1 * 16 + 16)
            for j in range(TPP):
                ins = v.bn_stats(out=stats[:, q1, j, :], in_=xin[:, q1, j, :])
            ins.then_inc(stats_set, 1)
            dve.wait_ge(stats_set, turn)
            dve.sem_inc(images_counted, 1)
            for j in range(TPP):
                ins = v.bn_aggr(out=moments[:, q1, j, :], in_=stats[:, q1, j, :])
            ins.then_inc(moments_set, 1)

        def scales(rnd, q, o):
            _, q1, turn = ahead(rnd, q, o)
            dve.wait_ge(std_set, turn)
            v.reciprocal(rstd[:, q1, :], std[:, q1, :]).then_inc(rstd_set, 1)
            dve.wait_ge(rstd_set, turn)
            dve.wait_ge(moments_set, turn)
            v.scalar_tensor_tensor(out=shift[:, q1, :], in0=moments[:, q1, :, 0], scalar=-1.0, in1=rstd[:, q1, :],
                                   op0=ALU.mult, op1=ALU.mult).then_inc(shift_set, 1)

        def gray_sums(rnd, q):
            _, q1, turn = ahead(rnd, q, -1)
            dve.wait_ge(xhat_act, turn)
            dve.wait_ge(xhat_pool, turn)
            if not (isinstance(rnd, int) and turn == 1):
                dve.wait_ge(gray_sum, turn - 1)
            for j in range(TPP):
                ins = v.scalar_tensor_tensor(out=weighted[:, j, :], in0=xin[:, q1, j, :], scalar=1.0, in1=gamma_row[:, :],
                                             op0=ALU.mult, op1=ALU.mult,
                                             accum_out=gray_tok[:, bass.ds(turn - 1, 1), j:j + 1].rearrange("p a b -> p (a b)"))
            ins.then_inc(gray_sum, 1)

        def image(rnd, q, first=False, last=False):
            if not (last and q == SLOTS - 1):
                statistics(rnd, q, 1)
            if not (first and q == 0):
                gray_sums(rnd, q)
            if not (last and q == SLOTS - 1):
                scales(rnd, q, 1)

        statistics(0, 0, 0)
        scales(0, 0, 0)
        dve.wait_ge(first_in, 16 * N_FIRST)
        for q in range(SLOTS):
            image(0, q, first=True)
        with dve.Fori(1, B // SLOTS - 1) as i:
            for q in range(SLOTS):
                image(i, q)
        for q in range(SLOTS):
            image(B // SLOTS - 1, q, last=True)
        gray_sums(B // SLOTS, 0)

        def absolute(dst, src):
            return v.scalar_tensor_tensor(out=dst, in0=src, scalar=-1.0, in1=src, op0=ALU.mult, op1=ALU.max)

        dve.wait_ge(gray_mm, 1)
        link(v.tensor_copy(beta_mean[:, :], bank[5][0:H, 0:1]))
        link(v.tensor_scalar(gray[:, 1:WD + 1, :].rearrange("h (k j) b -> h k b j", j=TPP),
                             bank[4][0:H, :].rearrange("h (k b j) -> h k b j", b=B, j=TPP),
                             beta_mean[:, 0:1], None, ALU.add))
        v.tensor_copy(gray[:, 0, :], gray[:, 2, :])
        v.tensor_copy(gray[:, WD + 1, :], gray[:, WD - 1, :]).then_inc(gray_set, 1)
        dve.wait_ge(gray_set, 1)
        link(v.tensor_tensor(gt[:, :, :], gray[:, 2:WD + 2, :], gray[:, 0:WD, :], ALU.subtract))
        absolute(gh[:, :, :], gt[:, :, :]).then_inc(gradh_set, 1)
        dve.wait_ge(gradh_set, 1)
        dve.wait_ge(diff_mm, 1)
        dve.wait_ge(norm_set, 1)
        link(v.tensor_scalar(norm[:, 0:1], norm[:, 0:1], NORM_MIN, None, ALU.max))
        link(v.tensor_scalar(norm[:, 1:2].bitcast(I32), norm[:, 0:1].bitcast(I32), 0x7F800000, None, ALU.bitwise_and))
        link(v.tensor_scalar(scale[:, 0:1], norm[:, 1:2], 1.0 / (TOP * K), None, ALU.mult))
        v.tensor_scalar(scale[:, 1:2], norm[:, 1:2], -1.0 / (TOP * K), None, ALU.mult)
        link(v.reciprocal(sk[:, :], scale[:, 0:1]))
        v.tensor_scalar(scale[:, 2:3], sk[:, :], 1.0 / K, None, ALU.mult)
        v.tensor_scalar(usual[:, :], norm[0:1, 1:2], NORM_MIN, None, ALU.is_le).then_inc(scale_set, 1)
        link(v.tensor_copy(gt[:, :, :].rearrange("h w b -> h (w b)"), bank[5][0:H, :]))
        link(absolute(gv[:, 1:WD + 1, :], gt[:, :, :]))
        link(v.tensor_copy(gv[:, 0, :], gv[:, 2, :]))
        link(v.tensor_copy(gv[:, WD + 1, :], gv[:, WD - 1, :]))
        half = WD // 2

        def weights(col, w0):
            return con[0:H, col + w0:col + w0 + half].unsqueeze(2).to_broadcast([H, half, B])

        for lo, w0 in ((0, 0), (half + 1, half)):
            dst = g4[:, 1, w0:w0 + half, :]
            v.tensor_tensor(gt[:, w0:w0 + half, :], gv[:, lo:lo + half, :], weights(C_WLO, w0), ALU.mult)
            ins = v.tensor_tensor(dst, gv[:, lo + 1:lo + 1 + half, :], weights(C_WHI, w0), ALU.mult)
        link(ins)
        link(v.tensor_tensor(g4[:, 1], g4[:, 1], gt[:, :, :], ALU.add))
        dve.wait_ge(rows_mm, 1)
        link(v.tensor_copy(g4[:, 0].rearrange("h w b -> h (w b)"), bank[4][0:H, :]))
        link(v.tensor_tensor(g4[:, 2], g4[:, 0], g4[:, 1], ALU.subtract))
        link(absolute(g4[:, 2], g4[:, 2]))
        poolw = con[0:H, C_POOLW:C_POOLW + WD].unsqueeze(2).to_broadcast([H, WD, B])
        for k in range(3):
            ins = v.tensor_tensor(g4[:, k], g4[:, k], poolw, ALU.mult)
        link(ins)
        link(v.tensor_reduce(pooled[:, 0:3, :], g4[:, 0:3, :, :].rearrange("h k w b -> h k b w"), AX, ALU.add))
        link(v.tensor_tensor(pooled[:, 3, :], pooled[:, 0, :], pooled[:, 1, :], ALU.add))
        v.tensor_scalar(pooled[:, 3, :], pooled[:, 3, :], 0.5, None, ALU.mult).then_inc(pooled_set, 1)
        dve.wait_ge(scores_mm, 1)
        v.tensor_copy(scores[:, :], bank[5][0:4, 0:B]).then_inc(scores_set, 1)
        dve.wait_ge(hid_mm, 1)
        v.tensor_scalar(hid1[:, :], bank[4][0:32, 0:B], mlpb1[:, 0:1], 0.0, ALU.add, ALU.max).then_inc(hid_set, 1)
        dve.wait_ge(logits_mm, 1)
        link(v.tensor_tensor(lg[:, 0:4], bank[5][0:B, 0:4], mlpb2[:, :], ALU.add))
        link(v.tensor_reduce(lg[:, 13:14], lg[:, 0:4], AX, ALU.max))
        v.tensor_scalar(lg[:, 12:13], lg[:, 13:14], -1.0, None, ALU.mult).then_inc(logits_set, 1)
        dve.wait_ge(exp_set, 1)
        link(v.tensor_reduce(lg[:, 14:15], lg[:, 4:8], AX, ALU.add))
        link(v.reciprocal(lg[:, 15:16], lg[:, 14:15]))
        link(v.tensor_scalar(lg[:, 8:12], lg[:, 4:8], lg[:, 15:16], None, ALU.mult))
        link(v.tensor_scalar(lg[:, 4:5], lg[:, 8:9], lg[:, 9:10], None, ALU.is_lt))
        link(v.tensor_scalar(lg[:, 5:7], lg[:, 10:12], lg[:, 9:10], None, ALU.is_le))
        link(v.tensor_tensor(lg[:, 7:8], lg[:, 5:6], lg[:, 6:7], ALU.mult))
        link(v.tensor_tensor(lg[:, 7:8], lg[:, 7:8], lg[:, 4:5], ALU.mult))
        v.tensor_scalar(diag[:, :], con[0:B, C_IDENT:C_IDENT + B], lg[:, 7:8], None, ALU.mult).then_inc(diag_set, 1)
        dve.wait_ge(mask_mm, 1)
        link(v.tensor_copy(mask[:, :], bank[7][:, 0:B]))
        dve.wait_ge(seq_set, 2 * B)

        def select(t0, t1):
            return v.copy_predicated(seq[:, t0:t1, :], mask[:, :].unsqueeze(1).to_broadcast([P, t1 - t0, B]),
                                     seq_v[:, t0:t1, :])

        select(0, EDGE)
        select(L - EDGE, L).then_inc(select_done, 1)

        dve.wait_ge(init_done, N_INIT)

        def add_output(j, d, ready, landed):
            dve.wait_ge(y_ready, ready)
            dve.wait_ge(tile_in[landed[0]], landed[1])
            kk = j if d == 0 else j * -1 + (NBLK - 1)
            t = tiles[:, bass.ds(kk, 1), :].rearrange("p a c -> p (a c)")
            v.tensor_tensor(t, Y[:, d * C:(d + 1) * C], t, ALU.add).then_inc(y_used, 1)

        def candidate(base, r, d):
            q, s, e = r // TB, r % TB, r % 2
            turn = base + (r + 1)
            at = (s * 2 + d) * 2 * B
            dve.wait_ge(reset_ready[d], turn)
            dve.wait_ge(hn_ready[d], turn)
            v.tensor_tensor_scan(cand[:, (2 * e + d) * 2 * B:(2 * e + d + 1) * 2 * B],
                                 rpair[:, e, 2 * B * d:2 * B * (d + 1)], NX[q][:, at:at + 2 * B], 0.0,
                                 ALU.mult, ALU.add).then_inc(cand_pre[d], 1)

        def new_state(base, r, d):
            e, cols = r % 2, slice(4 * B * d, 4 * B * (d + 1))
            turn = base + (r + 1)
            dve.wait_ge(cand_ready[d], turn)
            dve.wait_ge(update_ready[d], turn)
            if not (isinstance(base, int) and base + r == 0):
                dve.wait_ge(rec_ready[d], base + r)
            v.tensor_tensor_scan(state[:, r, cols], zquad[:, e, cols], rec[:, e, cols], 0.0,
                                 ALU.mult, ALU.add).then_inc(state_ready[d], 1)

        def split_state(base, r, d):
            e = r % 2
            new = state[:, r, 4 * B * d:4 * B * (d + 1)].rearrange("p (n k) -> p n k", k=4)
            dve.wait_ge(state_ready[d], base + (r + 1))
            v.tensor_scalar(h_hi[:, e, d * B:(d + 1) * B], new[:, :, 3], BIG, -1.0,
                            ALU.add, ALU.mult).then_inc(hi_ready[d], 1)
            v.scalar_tensor_tensor(out=h_lo[:, e, d * B:(d + 1) * B], in0=new[:, :, 3], scalar=BIG, in1=new[:, :, 2],
                                   op0=ALU.add, op1=ALU.add).then_inc(lo_ready[d], 1)

        def record_state(r, d):
            e = r % 2
            new = state[:, r, 4 * B * d:4 * B * (d + 1)].rearrange("p (n k) -> p n k", k=4)
            v.tensor_tensor(rec[:, 1 - e, 4 * B * d:4 * B * (d + 1)].rearrange("p (n k) -> p n k", k=4)[:, :, 1:3],
                            new[:, :, 2:3].to_broadcast([P, B, 2]),
                            signs[:, 0:2 * B].rearrange("p (n k) -> p n k", k=2), ALU.mult).then_inc(rec_ready[d], 1)

        def body(base, kblk, first, landed):
            share = (L - 2 * EDGE) // RING
            for r in range(RING):
                q, s = r // TB, r % TB
                candidate(base, r, 0)
                if not (first and r == 0):
                    record_state((r - 1) % RING, 1)
                if s in (3, 5) and not first:
                    add_output(kblk + (q - 2), s // 4, kblk + (q - 1), landed[q])
                if first:
                    ins = select(EDGE + r * share, EDGE + (r + 1) * share)
                    if r == RING - 1:
                        ins.then_inc(select_rest, 1)
                new_state(base, r, 0)
                candidate(base, r, 1)
                split_state(base, r, 0)
                record_state(r, 0)
                new_state(base, r, 1)
                split_state(base, r, 1)

        body(0, 0, True, None)
        with dve.Fori(1, NBLK // 8 + 1) as i:
            body(i * (2 * RING) - RING, i * 4 - 2, False, ((0, i * 64 - 32), (1, i * 64 - 32)))
            body(i * (2 * RING), i * 4, False, ((0, i * 64), (1, i * 64)))
        with dve.Fori(NBLK // 8 + 1, NBLK // 4) as i:
            body(i * (2 * RING) - RING, i * 4 - 2, False, ((0, 8 * NBLK), (1, 8 * NBLK)))
            body(i * (2 * RING), i * 4, False, ((0, 8 * NBLK), (1, 8 * NBLK)))
        body(L - RING, NBLK - 2, False, ((0, 8 * NBLK), (1, 8 * NBLK)))
        for k in (NBLK - 2, NBLK - 1):
            for d in range(2):
                add_output(k, d, k + 1, (k % 2, 8 * NBLK))

    ctx.close()


def kernel(x, L0_conv_ln_gamma, L0_conv_ln_beta, L0_conv_mlp_w1, L0_conv_mlp_b1, L0_conv_mlp_w2, L0_conv_mlp_b2,
           L0_conv_in_w, L0_conv_in_b, L0_conv_gru_wih_f, L0_conv_gru_whh_f, L0_conv_gru_bih_f, L0_conv_gru_bhh_f,
           L0_conv_gru_wih_b, L0_conv_gru_whh_b, L0_conv_gru_bih_b, L0_conv_gru_bhh_b, L0_conv_out_w, L0_conv_out_b):
    import numpy as np
    import concourse.bacc as bacc
    from concourse.bass_utils import run_bass_kernel_spmd

    def both(f, b):
        return np.stack([np.asarray(f), np.asarray(b)])

    def turned(a):
        return np.ascontiguousarray(np.swapaxes(np.asarray(a), -1, -2))

    def column(a):
        return np.asarray(a)[:, None]

    arrays = {
        "x": x, "gamma": column(L0_conv_ln_gamma), "beta": column(L0_conv_ln_beta),
        "w1t": turned(L0_conv_mlp_w1), "b1": column(L0_conv_mlp_b1), "w2t": turned(L0_conv_mlp_w2), "b2": np.asarray(L0_conv_mlp_b2)[None, :],
        "in_w": L0_conv_in_w, "in_b": turned(np.asarray(L0_conv_in_b).reshape(DI // P, P)),
        "wiht": turned(both(L0_conv_gru_wih_f, L0_conv_gru_wih_b)),
        "whht": turned(both(L0_conv_gru_whh_f, L0_conv_gru_whh_b)),
        "bih": both(L0_conv_gru_bih_f, L0_conv_gru_bih_b).reshape(2, 3, HID).transpose(2, 0, 1),
        "bhh": both(L0_conv_gru_bhh_f, L0_conv_gru_bhh_b).reshape(2, 3, HID).transpose(2, 0, 1),
        "outwt": turned(L0_conv_out_w), "out_b": column(L0_conv_out_b), "consts": shape_constants(),
    }
    nc = bacc.Bacc("TRN2", target_bir_lowering=False, num_devices=1)
    fed, aps = {}, []
    for name, a in arrays.items():
        a = np.ascontiguousarray(a)
        fed[f"in_{name}"] = a
        aps.append(nc.dram_tensor(f"in_{name}", a.shape, mybir.dt.from_np(a.dtype), kind="ExternalInput").ap())
    aps.append(nc.dram_tensor("out", (B, H, WD, C), F32, kind="ExternalOutput").ap())
    build(nc, *aps)
    got = run_bass_kernel_spmd(nc, [fed], core_ids=[0])
    return got.results[0]["out"]
```
